# Optimizing a Trainium2 kernel written in Bass

```python
import numpy as np
import jax
import jax.numpy as jnp

def _softmax(x, axis=-1):
    return jax.nn.softmax(x, axis=axis)

def _gelu(x):
    return jax.nn.gelu(x, approximate=True)

def _silu(x):
    return jax.nn.silu(x)

def _sigmoid(x):
    return jax.nn.sigmoid(x)

def _layernorm(x, axis=-1, eps=1e-05):
    m = jnp.mean(x, axis=axis, keepdims=True)
    v = jnp.var(x, axis=axis, keepdims=True)
    return (x - m) / jnp.sqrt(v + eps)

def _scatter_add(tgt, idx, src, axis=0):
    return tgt.at[idx].add(src)

def _segment_sum(src, seg, n):
    return jax.ops.segment_sum(src, seg, n)
kernel_name = 'mk_decoder_postln_d1_seqx_r8_3db201'

def setup_inputs(seed: int=0):
    np.random.seed(seed)
    _w = jnp.asarray

    def _rec_inputs():
        import jax
        import jax.numpy as jnp
        _rk = jax.random.key(seed)
        x = -0.0003929 + 0.9999 * jax.random.normal(jax.random.fold_in(_rk, 1), (16, 64, 512), jnp.float32)
        _lenS = 64 - jax.random.randint(jax.random.fold_in(_rk, 7), (16,), 0, max(1, 64 // 4) + 1, jnp.int32)
        _lenS2 = 64 - jax.random.randint(jax.random.fold_in(_rk, 8), (16,), 0, max(1, 64 // 4) + 1, jnp.int32)
        _ctx_1024P = jax.random.normal(jax.random.fold_in(_rk, 11), (16, 16, 128), jnp.float32)
        _ctx_1024c = jax.random.dirichlet(jax.random.fold_in(_rk, 511), 0.3 * jnp.ones((16,), jnp.float32), (16, 64))
        _ctx_1024t = jnp.einsum('bsk,bkd->bsd', _ctx_1024c, _ctx_1024P)
        _ctx_1024t = _ctx_1024t * jax.lax.rsqrt(jnp.mean(jnp.square(_ctx_1024t)) + 1e-12) * 0.953939
        ctx_1024 = -1.39393e-06 + 0.999914 * (_ctx_1024t + 0.3 * jax.random.normal(jax.random.fold_in(_rk, 611), (16, 64, 128), jnp.float32))
        return (x, ctx_1024)
    x, ctx_1024 = _rec_inputs()

    def _L0_attn_setup():
        import jax, jax.numpy as jnp
        import numpy as np
        import math
        B, L, D, H = (32, 64, 512, 32)
        HD = D // H
        key = jax.random.key(seed)
        ks = jax.random.split(key, 9)
        s = 1.0 / math.sqrt(D)
        return {'x': jax.random.normal(ks[0], (B, L, D), jnp.float32), 'Wq': jax.random.normal(ks[1], (D, D), jnp.float32) * s, 'bq': jax.random.normal(ks[2], (D,), jnp.float32) * s, 'Wk': jax.random.normal(ks[3], (D, D), jnp.float32) * s, 'bk': jax.random.normal(ks[4], (D,), jnp.float32) * s, 'Wv': jax.random.normal(ks[5], (D, D), jnp.float32) * s, 'bv': jax.random.normal(ks[6], (D,), jnp.float32) * s, 'Wo': jax.random.normal(ks[7], (D, D), jnp.float32) * s, 'bo': jax.random.normal(ks[8], (D,), jnp.float32) * s}
    _L0_attn_all = _L0_attn_setup()
    _L0_attn_in = {k: v for k, v in _L0_attn_all.items() if k in ('Wq', 'bq', 'Wk', 'bk', 'Wv', 'bv', 'Wo', 'bo')}
    del _L0_attn_all

    def _L0_xattn_setup():
        import jax, jax.numpy as jnp
        import numpy as np
        import math
        DIM_V = 64
        key = jax.random.key(seed)
        k1, k2, k3, k4, k5, k6 = jax.random.split(key, 6)
        B, C, N, M = (8, DIM_V, 512, 128)
        pcd_up = jax.random.normal(k1, (B, C, N), dtype=jnp.float32)
        pcd_down = jax.random.normal(k2, (B, C, M), dtype=jnp.float32)
        s = 1.0 / math.sqrt(C)
        Wq = jax.random.normal(k3, (C, C), dtype=jnp.float32) * s
        Wk = jax.random.normal(k4, (C, C), dtype=jnp.float32) * s
        Wv = jax.random.normal(k5, (C, C), dtype=jnp.float32) * s
        Wskip = jax.random.normal(k6, (C, C), dtype=jnp.float32) * s
        return {'pcd_up': pcd_up, 'pcd_down': pcd_down, 'Wq': Wq, 'Wk': Wk, 'Wv': Wv, 'Wskip': Wskip}
    _L0_xattn_all = _L0_xattn_setup()
    _L0_xattn_in = {k: v for k, v in _L0_xattn_all.items() if k in ('Wq', 'Wk', 'Wv', 'Wskip')}
    del _L0_xattn_all

    def _L0_ffn_setup():
        import jax, jax.numpy as jnp
        import numpy as np
        HID, BOT, RDIM, NSLOT, K, VB = (512, 64, 48, 128, 8, 32)
        TAU_LOW, TAU_HIGH, EARLY_EXIT = (0.5, 2.0, 0.05)

        def _uncertainty(h, Wu1, bu1, Wu2, bu2):
            var = jnp.var(h, axis=-1)
            log_var = jnp.log1p(var)
            norm_var = log_var / (jnp.mean(log_var) + 1e-06)
            learned = (jax.nn.gelu(h @ Wu1.T + bu1) @ Wu2.T + bu2)[..., 0]
            return jnp.clip(norm_var * 0.5 + jax.nn.sigmoid(learned) * 2.5, 0.0, 5.0)
        key = jax.random.key(seed)
        ks = jax.random.split(key, 12)
        B, S = (2, 256)
        return {'hidden_states': jax.random.normal(ks[0], (B, S, HID), dtype=jnp.float32), 'Wq': jax.random.normal(ks[1], (BOT, HID), dtype=jnp.float32) / np.sqrt(HID), 'Wr': jax.random.normal(ks[2], (RDIM, BOT), dtype=jnp.float32) / np.sqrt(BOT), 'aux_keys': jax.random.normal(ks[3], (NSLOT, BOT), dtype=jnp.float32) * 0.01, 'aux_values': jax.random.normal(ks[4], (NSLOT, HID), dtype=jnp.float32) * 0.02, 'Wvd': jax.random.normal(ks[5], (VB, HID), dtype=jnp.float32) * 0.1 / np.sqrt(HID), 'Wvu': jax.random.normal(ks[6], (HID, VB), dtype=jnp.float32) * 0.1 / np.sqrt(VB), 'Wu1': jax.random.normal(ks[7], (HID // 4, HID), dtype=jnp.float32) / np.sqrt(HID), 'bu1': jnp.zeros((HID // 4,), dtype=jnp.float32), 'Wu2': jax.random.normal(ks[8], (1, HID // 4), dtype=jnp.float32) * 0.01, 'bu2': jnp.zeros((1,), dtype=jnp.float32), 'gate_w1': jnp.float32(0.5), 'gate_bias': jnp.float32(-1.0), 'log_rel': jnp.zeros((NSLOT,), dtype=jnp.float32)}
    _L0_ffn_all = _L0_ffn_setup()
    _L0_ffn_in = {k: v for k, v in _L0_ffn_all.items() if k in ('Wq', 'Wr', 'aux_keys', 'aux_values', 'Wvd', 'Wvu', 'Wu1', 'bu1', 'Wu2', 'bu2', 'gate_w1', 'gate_bias', 'log_rel')}
    del _L0_ffn_all
    return {'x': x, 'ctx_1024': ctx_1024, 'L0_attn_Wq': _L0_attn_in['Wq'], 'L0_attn_bq': _L0_attn_in['bq'], 'L0_attn_Wk': _L0_attn_in['Wk'], 'L0_attn_bk': _L0_attn_in['bk'], 'L0_attn_Wv': _L0_attn_in['Wv'], 'L0_attn_bv': _L0_attn_in['bv'], 'L0_attn_Wo': _L0_attn_in['Wo'], 'L0_attn_bo': _L0_attn_in['bo'], 'L0_xattn_Wq': _L0_xattn_in['Wq'], 'L0_xattn_Wk': _L0_xattn_in['Wk'], 'L0_xattn_Wv': _L0_xattn_in['Wv'], 'L0_xattn_Wskip': _L0_xattn_in['Wskip'], 'L0_ffn_Wq': _L0_ffn_in['Wq'], 'L0_ffn_Wr': _L0_ffn_in['Wr'], 'L0_ffn_aux_keys': _L0_ffn_in['aux_keys'], 'L0_ffn_aux_values': _L0_ffn_in['aux_values'], 'L0_ffn_Wvd': _L0_ffn_in['Wvd'], 'L0_ffn_Wvu': _L0_ffn_in['Wvu'], 'L0_ffn_Wu1': _L0_ffn_in['Wu1'], 'L0_ffn_bu1': _L0_ffn_in['bu1'], 'L0_ffn_Wu2': _L0_ffn_in['Wu2'], 'L0_ffn_bu2': _L0_ffn_in['bu2'], 'L0_ffn_gate_w1': _L0_ffn_in['gate_w1'], 'L0_ffn_gate_bias': _L0_ffn_in['gate_bias'], 'L0_ffn_log_rel': _L0_ffn_in['log_rel']}

def reference(x, ctx_1024, L0_attn_Wq, L0_attn_bq, L0_attn_Wk, L0_attn_bk, L0_attn_Wv, L0_attn_bv, L0_attn_Wo, L0_attn_bo, L0_xattn_Wq, L0_xattn_Wk, L0_xattn_Wv, L0_xattn_Wskip, L0_ffn_Wq, L0_ffn_Wr, L0_ffn_aux_keys, L0_ffn_aux_values, L0_ffn_Wvd, L0_ffn_Wvu, L0_ffn_Wu1, L0_ffn_bu1, L0_ffn_Wu2, L0_ffn_bu2, L0_ffn_gate_w1, L0_ffn_gate_bias, L0_ffn_log_rel):
    import jax
    import jax.numpy as jnp

    def _L0_attn_ref(x, Wq, bq, Wk, bk, Wv, bv, Wo, bo):
        import jax, jax.numpy as jnp
        import numpy as np
        import math
        B, L, D, H = (32, 64, 512, 32)
        HD = D // H
        b, l, d = x.shape
        h, hd = (H, HD)
        q = (x @ Wq.T + bq).reshape(b, l, h, hd).transpose(0, 2, 1, 3)
        k = (x @ Wk.T + bk).reshape(b, l, h, hd).transpose(0, 2, 1, 3)
        v = (x @ Wv.T + bv).reshape(b, l, h, hd).transpose(0, 2, 1, 3)
        scores = jnp.einsum('bhqd,bhkd->bhqk', q, k) / math.sqrt(hd)
        causal = jnp.tril(jnp.ones((l, l), bool))
        scores = jnp.where(causal, scores, -jnp.inf)
        att = jax.nn.softmax(scores, axis=-1)
        out = jnp.einsum('bhqk,bhkd->bhqd', att, v)
        out = out.transpose(0, 2, 1, 3).reshape(b, l, d)
        return out @ Wo.T + bo

    def _L0_xattn_ref(pcd_up, pcd_down, Wq, Wk, Wv, Wskip):
        import jax, jax.numpy as jnp
        import numpy as np
        import math
        DIM_V = 64
        q = jnp.einsum('oc,bcn->bon', Wq, pcd_up)
        k = jnp.einsum('oc,bcm->bom', Wk, pcd_down)
        v = jnp.einsum('oc,bcm->bom', Wv, pcd_down)
        C = q.shape[1]
        scale = jnp.sqrt(jnp.asarray(C, dtype=q.dtype))
        energy = jnp.einsum('bcn,bcm->bnm', q, k) / scale
        attention = jax.nn.softmax(energy, axis=-1)
        x = jnp.einsum('bnm,bcm->bcn', attention, v)
        skip = jnp.einsum('oc,bcn->bon', Wskip, pcd_up)
        return skip + x

    def _L0_ffn_ref(hidden_states, Wq, Wr, aux_keys, aux_values, Wvd, Wvu, Wu1, bu1, Wu2, bu2, gate_w1, gate_bias, log_rel):
        import jax, jax.numpy as jnp
        import numpy as np
        HID, BOT, RDIM, NSLOT, K, VB = (512, 64, 48, 128, 8, 32)
        TAU_LOW, TAU_HIGH, EARLY_EXIT = (0.5, 2.0, 0.05)

        def _uncertainty(h, Wu1, bu1, Wu2, bu2):
            var = jnp.var(h, axis=-1)
            log_var = jnp.log1p(var)
            norm_var = log_var / (jnp.mean(log_var) + 1e-06)
            learned = (jax.nn.gelu(h @ Wu1.T + bu1) @ Wu2.T + bu2)[..., 0]
            return jnp.clip(norm_var * 0.5 + jax.nn.sigmoid(learned) * 2.5, 0.0, 5.0)
        query = hidden_states @ Wq.T
        rq = query @ Wr.T
        rk = aux_keys @ Wr.T
        router_scores = jnp.einsum('bsr,nr->bsn', rq, rk) / np.sqrt(RDIM) + log_rel
        top_scores, top_idx = jax.lax.top_k(router_scores, K)
        sel_keys = aux_keys[top_idx]
        attn = jnp.einsum('bsd,bskd->bsk', query, sel_keys) / np.sqrt(BOT) + log_rel[top_idx]
        w = jax.nn.softmax(attn, axis=-1)
        sel_vals = aux_values[top_idx]
        aux_out = jnp.einsum('bsk,bskh->bsh', w, sel_vals)
        aux_out = aux_out @ Wvd.T @ Wvu.T
        u = _uncertainty(hidden_states, Wu1, bu1, Wu2, bu2)
        u_norm = jnp.clip((u - TAU_LOW) / (TAU_HIGH - TAU_LOW), 0.0, 1.0)
        gate = jax.nn.sigmoid(gate_w1 * u_norm + gate_bias)
        gate = jnp.where(gate < EARLY_EXIT, 0.0, gate)
        return hidden_states + gate[..., None] * aux_out
    x = _layernorm(x + _L0_attn_ref(x, L0_attn_Wq, L0_attn_bq, L0_attn_Wk, L0_attn_bk, L0_attn_Wv, L0_attn_bv, L0_attn_Wo, L0_attn_bo), axis=-1)
    x = _layernorm(x + _L0_xattn_ref(x, ctx_1024, L0_xattn_Wq, L0_xattn_Wk, L0_xattn_Wv, L0_xattn_Wskip), axis=-1)
    x = _layernorm(x + _L0_ffn_ref(x, L0_ffn_Wq, L0_ffn_Wr, L0_ffn_aux_keys, L0_ffn_aux_values, L0_ffn_Wvd, L0_ffn_Wvu, L0_ffn_Wu1, L0_ffn_bu1, L0_ffn_Wu2, L0_ffn_bu2, L0_ffn_gate_w1, L0_ffn_gate_bias, L0_ffn_log_rel), axis=-1)
    return x

_drawn_inputs = setup_inputs


def setup_inputs(seed=0):
    import zlib

    import numpy as np

    out = dict(_drawn_inputs(seed))
    spreads = {'L0_ffn_bu1': (0.0, 2.0), 'L0_ffn_log_rel': (0.0, 2.0)}
    factors = {'L0_attn_bq': 5.279,
     'L0_attn_bk': 64.0,
     'L0_ffn_Wq': 54.25,
     'L0_ffn_Wr': 64.0,
     'L0_ffn_aux_keys': 53.96,
     'L0_ffn_aux_values': 52.602,
     'L0_ffn_Wvd': 53.147,
     'L0_ffn_Wvu': 52.101,
     'L0_ffn_Wu1': 64.0,
     'L0_ffn_Wu2': 64.0}
    for name, (base, spread) in spreads.items():
        noise = np.random.default_rng([zlib.crc32(name.encode()), seed]).standard_normal(out[name].shape)
        drawn = base * np.exp(spread * noise) if base else spread * noise
        out[name] = jnp.asarray(drawn.astype(out[name].dtype))
    for name, factor in factors.items():
        out[name] = (out[name] * factor).astype(out[name].dtype)
    return out
```

```python
from contextlib import ExitStack

import numpy as np
import concourse.bass as bass
from concourse import mybir

F32 = mybir.dt.float32
F32R = mybir.dt.float32r
BF16 = mybir.dt.bfloat16
ALU = mybir.AluOpType
ACT = mybir.ActivationFunctionType
AX = mybir.AxisListType

P = 128
B, L, D = 16, 64, 512
H, HD = 32, 16
M = 128
BOT, RDIM, NSLOT, TOPK, VB, UH = 64, 48, 128, 8, 32, 128
NTOK = B * L
NT = NTOK // P
PB = P // L
KC = D // P
HG = D // P
HPG = P // HD
NP2 = H // 2
GT = 2
GW = GT * P
NG = NT // GT
VW = 2 * HD + 2
NF = 2 * NSLOT + UH
EPS = 1e-5
FAR = -1e30
TAKEN = -3e38
GELU_C = float(np.sqrt(2 / np.pi))
GELU_A = 0.044715
TAU_LOW, TAU_HIGH, EARLY_EXIT = 0.5, 2.0, 0.05
SPLIT = ((0, 0), (0, 1), (1, 0))


def projection_fills(i):
    g = i // 2 + 1
    if i < 0 or g >= NG:
        return [None] * HG
    return [("K" if i % 2 == 0 else "Q", g, hg) for hg in range(HG)]


def tensor_units():
    units = [("K", 0, hg) for hg in range(HG)] + [("Q", 0, hg) for hg in range(HG)]
    units += [("G",), ("kk", 0), ("kk", 1), ("vt", 0), ("vt", 1), ("rk1",), ("rk2",), ("C", 0), ("C", 1),
              ("a1",), ("U",), ("V", 0)]
    for i in range(NT + 1):
        t, u, w = i, i - 1, i - 2
        at, xa, ff = t < NT, 0 <= u, 0 <= w
        q = projection_fills(i)
        units += [("S", t, 0), ("S", t, 1)] if at else []
        units += [("bo",)] if t == 0 else []
        units += [("E", u, 0)] if xa else []
        units += [("T", t, 0)] if at else []
        units += [("E", u, 1)] if xa else []
        units += [("T", t, 1)] if at else []
        units += [("V", t + 1)] if t + 1 < NT else []
        units += [("PV", t, 0), ("S", t, 2), ("PV", t, 1), ("S", t, 3)] if at else []
        units += [("X", u, 0)] if xa else []
        units += [q[0]] if q[0] else []
        units += [("WT", w)] if ff else []
        units += [("T", t, 2)] if at else []
        units += [("X", u, 1)] if xa else []
        units += [("T", t, 3)] if at else []
        units += [("R", u)] if xa else []
        units += [q[1]] if q[1] else []
        units += [("PV", t, 2), ("PV", t, 3)] if at else []
        units += [q[2]] if q[2] else []
        units += [("OT", t)] if at else []
        units += [("HT", u)] if xa else []
        units += [q[3]] if q[3] else []
        units += [("WO", t)] if at else []
        units += [("F", u)] if xa else []
    units += [("mean",), ("AUX", 0), ("AUX", 1), ("WT", NT - 1)] + [("AUX", j) for j in range(2, NT)]
    return units


BANKS = {"scores": (0, 1), "turned": (2, 3), "products": (4, 5)}
CLASS_OF = {"S": "scores", "E": "scores", "T": "turned", "X": "turned", "OT": "turned", "HT": "turned",
            "WT": "turned"}


def place_units(units):
    place, turn, uses = {}, {c: 0 for c in BANKS}, {}
    for key in units:
        if key[0] == "PV":
            continue
        c = CLASS_OF.get(key[0], "products")
        bank = BANKS[c][turn[c] % len(BANKS[c])]
        turn[c] += 1
        place[key] = (bank, uses.get(bank, 0))
        uses[bank] = uses.get(bank, 0) + 1
    return place


def decoder_block(nc, a, out):
    units = tensor_units()
    place = place_units(units)

    with ExitStack() as ctx:
        def sb(name, shape, dt=F32):
            return ctx.enter_context(nc.sbuf_tensor(name, shape, dt))

        def sem(name):
            return ctx.enter_context(nc.semaphore(name))

        ps = [ctx.enter_context(nc.psum_tensor(f"bank{n}", [P, 512], F32)) for n in range(6)]
        o_ps = [ctx.enter_context(nc.psum_tensor(f"attn_out{n}", [P, 512], F32)) for n in range(2)]
        o_view = [o[:, 0:NP2 // 2 * VW].rearrange("p (n v) -> p n v", v=VW) for o in o_ps]

        ident = sb("ident", [P, P])
        ident_b = sb("ident_b", [P, P], BF16)
        causal = sb("causal", [P, HPG, L], BF16)
        ones = sb("ones", [P, P])
        norm_c = sb("norm_c", [P, 3])
        wk = [sb(f"wk{n}", [P, KC, D], F32R) for n in range(2)]
        wq = [sb(f"wq{n}", [P, KC, D], F32R) for n in range(2)]
        wv = [sb(f"wv{n}", [P, KC, D], F32R) for n in range(2)]
        wo = [sb(f"wo{n}", [P, KC, D], F32R) for n in range(2)]
        bias_qkv = sb("bias_qkv", [P, 3, HG])
        bo_all = sb("bo_all", [P, D])
        kk_bd = sb("kk_bd", [P, NT, PB, M])
        vt = sb("vt", [P, NT, P])
        bd_skip = sb("bd_skip", [P, P])
        bd_g = sb("bd_g", [P, P])
        bd_v = sb("bd_v", [P, P])
        cw = [sb(f"cw{n}", [P, KC, NF], F32R) for n in range(2)]
        bias_f = sb("bias_f", [P, NF])
        wu2 = sb("wu2", [P, UH])
        gate_c = sb("gate_c", [P, 3])
        hgate_c = sb("hgate_c", [P, 3])
        u_val = sb("u_val", [P, D])

        xt = [[sb(f"xt{s}{n}", [P, KC, GW], F32R) for n in range(2)] for s in range(2)]
        kt = sb("kt", [P, 2, GT, HG * PB, L])
        qt = sb("qt", [P, HG, GW])
        k_bd = sb("k_bd", [P, HG * PB, HPG, L])
        v_bd = sb("v_bd", [P, 2, PB, NP2, VW])
        smax = sb("smax", [P, 2, HPG])
        pr = sb("pr", [P, 2, HPG, L])
        pt = sb("pt", [P, 2, 4, P])
        o_rden = sb("o_rden", [P, 2, NP2 // 2, 2])
        on = sb("on", [P, D])
        ot = [sb(f"ot{n}", [P, KC, P], F32R) for n in range(2)]
        xs = sb("xs", [P, 2, D])
        st = sb("st", [P, 3, NT, 6])
        mv = sb("mv", [P, 3, NT, 2])
        ve = sb("ve", [P, 3, NT])
        rs = sb("rs", [P, 3, NT])
        emax = sb("emax", [P, 2, 4])
        enb = sb("enb", [P, 2, 4])
        esum = sb("esum", [P, 2, 4])
        erd = sb("erd", [P, 2, 4])
        pe2 = sb("pe2", [P, 2, 4, P])
        pt2 = sb("pt2", [P, PB, KC, P])
        h_all = sb("h_all", [P, NT, D])
        ht = [sb(f"ht{n}", [P, KC, P], F32R) for n in range(2)]
        fs = sb("fs", [P, NF])
        m8 = sb("m8", [P, TOPK])
        rep = sb("rep", [P, NSLOT])
        am = sb("am", [P, NSLOT])
        amx = sb("amx", [P, 2])
        wts = sb("wts", [P, NSLOT])
        sq = sb("sq", [P, UH])
        th = sb("th", [P, UH])
        wt = sb("wt", [P, NT, P])
        wsum = sb("wsum", [P, NT])
        lrn = sb("lrn", [P, NT])
        vh = sb("vh", [P, 2, NT])
        lv = sb("lv", [P, NT])
        lsum = sb("lsum", [P, 1])
        rmean = sb("rmean", [P, 2])
        ga = sb("ga", [P, 10, NT])
        gs = sb("gs", [P, NT])

        w_raw = [h_all[:, 4 * n:4 * n + 4, :] for n in range(2)]
        x_raw = [pt[:].rearrange("p s i q -> p (s i q)").rearrange("p (c n) -> p c n", c=KC)] * 2 + \
                [h_all[:, NT - 2:NT].rearrange("p t n -> p (t n)").rearrange("p (c n) -> p c n", c=KC)] * (NG - 2)
        ctx_raw = pt2[:].rearrange("p b k n -> p (b k) n")
        wu1_raw, av_raw = pe2[:, 0], pe2[:, 1]
        wvu_raw = on[0:VB, :]
        fq = u_val[0:BOT, :]
        small = wt[:].rearrange("p t n -> p (t n)")
        xq_raw, xk_raw = small[0:L, 0:64], small[0:L, 64:128]
        wr_raw, wrt_raw = small[0:RDIM, 128:192], small[0:BOT, 192:240]
        akt_raw = small[0:BOT, 240:368]
        wvd_raw = small[:, 368:496].rearrange("p (c n) -> p c n", c=KC)
        rk1 = small[0:RDIM, 496:624]
        a1t = pr[0:VB, 0].rearrange("p h k -> p (h k)")[:, 0:P]
        rkk = pr[0:BOT, 1].rearrange("p h k -> p (h k)")[:, 0:2 * NSLOT]

        filled = [sem(f"filled{n}") for n in range(6)]
        drained = [sem(f"drained{n}") for n in range(6)]
        ld_w = {n: sem(f"ld_{n}") for n in ("wk", "wq", "wv", "wo")}
        ld_x = sem("ld_x")
        ld_xs = [sem(f"ld_xs{n}") for n in range(2)]
        ld_bias = sem("ld_bias")
        ld_bo = sem("ld_bo")
        ld_xa = sem("ld_xa")
        ld_ff = sem("ld_ff")
        c_bd = sem("c_bd")
        c_ident = sem("c_ident")
        c_causal = sem("c_causal")
        c_norm = sem("c_norm")
        c_kk = sem("c_kk")
        c_ones = sem("c_ones")
        k_bd_zeroed = sem("k_bd_zeroed")
        v_bd_zeroed = sem("v_bd_zeroed")
        w_hi, w_lo = ({n: sem(f"{n}_{half}") for n in ld_w} for half in ("hi", "lo"))
        x_hi, x_lo = sem("x_hi"), sem("x_lo")
        wu1_hi, wu1_lo = sem("wu1_hi"), sem("wu1_lo")
        c_hi = sem("c_hi")
        skip_ready = sem("skip_ready")
        hgate_ready = sem("hgate_ready")
        k_bd_loaded = sem("k_bd_loaded")
        smax_ready = sem("smax_ready")
        probs_ready = sem("probs_ready")
        pv_done = sem("pv_done")
        o_ready = sem("o_ready")
        oh_ready = sem("oh_ready")
        xb_ready = sem("xb_ready")
        stat = [sem(f"stat{n}") for n in range(3)]
        rstd = [sem(f"rstd{n}") for n in range(3)]
        x1_ready = sem("x1_ready")
        e_max = sem("e_max")
        e_norm = sem("e_norm")
        hh_ready = sem("hh_ready")
        sq_ready = sem("sq_ready")
        th_in, th_ready = sem("th_in"), sem("th_ready")
        am_ready, w_ready = sem("am_ready"), sem("w_ready")
        lrn_ready = sem("lrn_ready")
        lv_in, lv_ready = sem("lv_in"), sem("lv_ready")
        g_tanh1, g_mid, g_tanh2 = sem("g_tanh1"), sem("g_mid"), sem("g_tanh2")
        y_ready = sem("y_ready")
        stored = sem("stored")
        dve_chain, pool_chain = sem("dve_chain"), sem("pool_chain")
        N_XA, N_FF = 3 + 2 * PB, 8 + 4 + 3

        def bank(key):
            return ps[place[key][0]]

        def wait_filled(eng, key):
            eng.wait_ge(filled[place[key][0]], place[key][1] + 1)

        def wait_drained(eng, key):
            eng.wait_ge(drained[place[key][0]], place[key][1] + 1)

        def is_drained(key):
            return drained[place[key][0]]

        block = ctx.enter_context(nc.Block())

        @block.sync
        def _(sp):
            def load_weight(name, raw):
                sp.dma_start(raw, a[name + "_t"].rearrange("(c p) o -> p c o", p=P)).then_inc(ld_w[name], 16)

            def load_xt(g):
                if g:
                    sp.wait_ge(x_lo, g)
                if g == 2:
                    sp.wait_ge(w_lo["wo"], 1)
                    wait_filled(sp, ("bo",))
                sp.dma_start(x_raw[g], a["x_t"].rearrange("(c p) n -> p c n", p=P)[:, :, g * GW:(g + 1) * GW]
                             ).then_inc(ld_x, 16)

            def load_xs(t):
                if t >= 2:
                    wait_filled(sp, ("R", t - 2))
                sp.dma_start(xs[:, t % 2, :], a["x"][t * P:(t + 1) * P, :]).then_inc(ld_xs[t % 2], 16)

            def load_k_blocks(t):
                g = t // GT
                for hg in range(HG):
                    wait_drained(sp, ("K", g, hg))
                if t:
                    wait_filled(sp, ("S", t - 1, HG - 1))
                else:
                    sp.wait_ge(k_bd_zeroed, 1)
                for j in range(HPG):
                    rows = slice(j * HD, (j + 1) * HD)
                    sp.dma_start(k_bd[rows, :, j, :], kt[rows, g % 2, t % GT]).then_inc(k_bd_loaded, 16)

            load_weight("wk", w_raw[0])
            load_xt(0)
            load_weight("wq", w_raw[1])
            for n, name in enumerate(("bq", "bk", "bv")):
                sp.dma_start(bias_qkv[:, n, :], a[name]).then_inc(ld_bias, 16)
            sp.dma_start(xq_raw, a["xa_wq"]).then_inc(ld_xa, 16)
            sp.dma_start(xk_raw, a["xa_wk"]).then_inc(ld_xa, 16)
            sp.dma_start(ctx_raw, a["ctx"].rearrange("(t p) m -> p t m", p=P)).then_inc(ld_xa, 16)
            sp.wait_ge(c_bd, 1)
            for b in range(PB):
                blk = slice(b * L, (b + 1) * L)
                sp.dma_start(bd_v[blk, blk], a["xa_wv_t"]).then_inc(ld_xa, 16)
                sp.dma_start(bd_skip[blk, blk], a["xa_ws_t"]).then_inc(ld_xa, 16)
            for dst, name in ((fq, "ff_wq"), (wr_raw, "ff_wr"), (wrt_raw, "ff_wr_t"), (akt_raw, "ff_ak_t"),
                              (av_raw, "ff_av_t"), (wvd_raw, "ff_wvd_t"), (wvu_raw, "ff_wvu_t"),
                              (wu1_raw, "ff_wu1_t")):
                src = a[name]
                if len(dst.shape) == 3:
                    src = src.rearrange("(c p) n -> p c n", p=P)
                sp.dma_start(dst, src).then_inc(ld_ff, 16)
            for n, name in enumerate(("log_rel", "log_rel", "bu1", "wu2")):
                dst = bias_f[:, n * NSLOT:(n + 1) * NSLOT] if n < 3 else wu2[:]
                sp.dma_start(dst, a[name].to_broadcast([P, NSLOT])).then_inc(ld_ff, 16)
            for n, name in enumerate(("bu2", "gate_w1", "gate_bias")):
                sp.dma_start(gate_c[:, n:n + 1], a[name].to_broadcast([P, 1])).then_inc(ld_ff, 16)
            sp.wait_ge(w_lo["wk"], 1)
            load_weight("wv", w_raw[0])
            load_k_blocks(0)
            sp.wait_ge(w_lo["wq"], 1)
            load_weight("wo", w_raw[1])
            sp.dma_start(bo_all[:], a["bo"].to_broadcast([P, D])).then_inc(ld_bo, 16)
            load_xt(1)
            load_xs(0)
            load_xs(1)
            for i in range(NT):
                if i % 2 == 0 and i // 2 + 2 < NG:
                    load_xt(i // 2 + 2)
                if i + 1 < NT:
                    load_k_blocks(i + 1)
                    if i >= 1:
                        load_xs(i + 1)
            for t in range(NT):
                sp.wait_ge(y_ready, t + 1)
                sp.dma_start(out[t * P:(t + 1) * P, :], h_all[:, t, :]).then_inc(stored, 16)
            sp.wait_ge(stored, 16 * NT)

        @block.gpsimd
        def _(pool):
            chain = [0]

            def link(ins):
                chain[0] += 1
                ins.then_inc(pool_chain, 1)
                pool.wait_ge(pool_chain, chain[0])

            nc.gpsimd.memset(bd_g[:], 0.0)
            nc.gpsimd.memset(bd_v[:], 0.0)
            nc.gpsimd.memset(bd_skip[:], 0.0).then_inc(c_bd, 1)
            link(nc.gpsimd.memset(ident[:], 0.0))
            link(nc.gpsimd.affine_select(out=ident[:], in_=ident[:], compare_op=ALU.not_equal, fill=1.0,
                                         base=0, pattern=[[-1, P]], channel_multiplier=1))
            nc.gpsimd.tensor_copy(ident_b[:], ident[:]).then_inc(c_ident, 1)
            nc.gpsimd.memset(norm_c[:, 0:1], EPS)
            nc.gpsimd.memset(norm_c[:, 1:2], EPS / 4)
            nc.gpsimd.memset(norm_c[:, 2:3], -0.5).then_inc(c_norm, 1)

            def split_x(g):
                pool.wait_ge(x_hi, g + 1)
                nc.gpsimd.tensor_tensor(xt[g % 2][1][:], x_raw[g], xt[g % 2][0][:].bitcast(F32),
                                        ALU.subtract).then_inc(x_lo, 1)

            split_x(0)
            nc.gpsimd.memset(kk_bd[:], 0.0).then_inc(c_kk, 1)
            link(nc.gpsimd.memset(causal[:], 0.0))
            for b in range(PB):
                rows = causal[b * L:(b + 1) * L]
                nc.gpsimd.affine_select(out=rows, in_=rows, compare_op=ALU.is_ge, fill=FAR, base=0,
                                        pattern=[[0, HPG], [-1, L]], channel_multiplier=1).then_inc(c_causal, 1)
                pool.wait_ge(c_causal, b + 1)
            nc.gpsimd.memset(ones[:], 1.0).then_inc(c_ones, 1)
            pool.wait_ge(c_norm, 1)

            def split_weight(name, halves, raw):
                pool.wait_ge(w_hi[name], 1)
                for c in range(KC):
                    last = nc.gpsimd.tensor_tensor(halves[1][:, c, :], raw[:, c, :], halves[0][:, c, :].bitcast(F32),
                                                   ALU.subtract)
                last.then_inc(w_lo[name], 1)

            def add_bias(t):
                pool.wait_ge(ld_xs[t % 2], 16 * (t // 2 + 1))
                if t == 0:
                    wait_drained(pool, ("bo",))
                nc.gpsimd.tensor_tensor(xs[:, t % 2, :], xs[:, t % 2, :], bo_all[:], ALU.add).then_inc(xb_ready, 1)

            def inv_std(n, t):
                eps = norm_c[:, 1:2] if n == 2 else norm_c[:, 0:1]
                pool.wait_ge(stat[n], t + 1)
                link(nc.gpsimd.tensor_tensor(ve[:, n, t:t + 1], mv[:, n, t, 1:2], eps, ALU.add))
                nc.gpsimd.tensor_tensor(rs[:, n, t:t + 1], ve[:, n, t:t + 1], norm_c[:, 2:3],
                                        ALU.pow).then_inc(rstd[n], 1)

            split_weight("wv", wv, w_raw[0])
            split_x(1)
            split_weight("wo", wo, w_raw[1])
            for i in range(NT + 1):
                if i >= 1:
                    inv_std(0, i - 1)
                if i < NT:
                    add_bias(i)
                if i >= 1:
                    inv_std(1, i - 1)
                if i % 2 == 1 and (i + 1) // 2 + 1 < NG:
                    split_x((i + 1) // 2 + 1)
            for t in range(NT):
                inv_std(2, t)

        @block.scalar
        def _(act):
            def split_weight(name, halves, raw):
                act.wait_ge(ld_w[name], 16)
                for c in range(KC):
                    last = nc.scalar.copy(halves[0][:, c, :], raw[:, c, :])
                last.then_inc(w_hi[name], 1)

            def split_x(g):
                act.wait_ge(ld_x, 16 * (g + 1))
                if g >= 2:
                    wait_filled(act, ("V", GT * (g - 1) - 1))
                nc.scalar.copy(xt[g % 2][0][:], x_raw[g]).then_inc(x_hi, 1)

            def k_to_sbuf(g, hg):
                key = ("K", g, hg)
                wait_filled(act, key)
                if (g, hg) == (0, 0):
                    act.wait_ge(ld_bias, 48)
                if g >= 2 and hg == 0:
                    act.wait_ge(k_bd_loaded, 16 * HPG * GT * (g - 1))
                nc.scalar.activation(kt[:, g % 2, :, hg * PB:(hg + 1) * PB, :].rearrange("p t b k -> p t (b k)"),
                                     bank(key)[:, 0:GW].rearrange("p (t n) -> p t n", t=GT), ACT.Identity,
                                     bias=bias_qkv[:, 1, hg:hg + 1]).then_inc(is_drained(key), 1)

            def v_to_blocks(t):
                key = ("V", t)
                wait_filled(act, key)
                if t == 0:
                    act.wait_ge(v_bd_zeroed, 1)
                if t >= 2:
                    act.wait_ge(pv_done, HG * (t - 1))
                for b in range(PB):
                    for h in range(2):
                        src = bank(key)[b * L:(b + 1) * L, :].rearrange("p (n h d) -> p n h d", h=2, d=HD)[:, :, h, :]
                        dst = v_bd[h * L:(h + 1) * L, t % 2, b, :, h * HD:(h + 1) * HD]
                        last = nc.scalar.copy(dst, src)
                last.then_inc(is_drained(key), 1)

            def exp_scores(t, hg):
                wait_drained(act, ("S", t, hg))
                u = HG * t + hg
                nc.scalar.activation(pr[:, u % 2], pr[:, u % 2], ACT.Exp, scale=HD ** -0.5).then_inc(probs_ready, 1)

            def probs_to_sbuf(t, hg):
                key, u = ("T", t, hg), HG * t + hg
                wait_filled(act, key)
                if u == 0:
                    act.wait_ge(x_lo, 2)
                if u >= 2:
                    act.wait_ge(pv_done, u - 1)
                nc.scalar.copy(pt[:, u % 2], bank(key)[:].rearrange("p (i q) -> p i q", i=4)
                               ).then_inc(is_drained(key), 1)

            def o_upper(t):
                key = ("OT", t)
                wait_filled(act, key)
                if t:
                    wait_filled(act, ("WO", t - 1))
                nc.scalar.copy(ot[0][:], bank(key)[:].rearrange("p (c q) -> p c q", c=KC)).then_inc(oh_ready, 1)

            def h_upper(u):
                key = ("HT", u)
                wait_filled(act, key)
                if u:
                    wait_filled(act, ("F", u - 1))
                nc.scalar.copy(ht[0][:], bank(key)[:].rearrange("p (c q) -> p c q", c=KC)).then_inc(hh_ready, 1)

            def exp_energy(u, j):
                key = ("E", u, j)
                act.wait_ge(e_max, 2 * u + j + 1)
                if u:
                    wait_filled(act, ("X", u - 1, j))
                for k in range(4):
                    last = nc.scalar.activation(pe2[:, j, k, :], bank(key)[:, k * M:(k + 1) * M], ACT.Exp,
                                                bias=enb[:, j, k:k + 1], scale=L ** -0.5,
                                                accum_out=esum[:, j, k:k + 1])
                last.then_inc(is_drained(key), 1)

            def energy_to_sbuf(u, j):
                key = ("X", u, j)
                wait_filled(act, key)
                if u and j == 0:
                    wait_filled(act, ("R", u - 1))
                nc.scalar.copy(pt2[:, :, 2 * j:2 * j + 2, :].rearrange("p b n q -> p n b q"),
                               bank(key)[:].rearrange("p (n b q) -> p n b q", n=2, b=PB)
                               ).then_inc(is_drained(key), 1)

            def gelu_square(w):
                wait_drained(act, ("F", w))
                nc.scalar.activation(sq[:], fs[:, 2 * NSLOT:NF], ACT.Square).then_inc(sq_ready, 1)

            def top8_exp(w):
                act.wait_ge(th_in, w + 1)
                nc.scalar.activation(th[:], sq[:], ACT.Tanh, scale=GELU_C).then_inc(th_ready, 1)
                act.wait_ge(am_ready, w + 1)
                if w:
                    wait_filled(act, ("WT", w - 1))
                nc.scalar.activation(wts[:], am[:], ACT.Exp, bias=amx[:, 1:2], accum_out=wsum[:, w:w + 1]
                                     ).then_inc(w_ready, 1)

            def weights_to_sbuf(w):
                key = ("WT", w)
                wait_filled(act, key)
                nc.scalar.copy(wt[:, w, :], bank(key)[:, 0:P]).then_inc(is_drained(key), 1)

            split_weight("wk", wk, w_raw[0])
            split_x(0)
            split_weight("wq", wq, w_raw[1])
            for hg in range(HG):
                k_to_sbuf(0, hg)
            act.wait_ge(ld_ff, 16 * N_FF)
            nc.scalar.copy(cw[0][:, :, 2 * NSLOT:NF], wu1_raw).then_inc(wu1_hi, 1)
            split_weight("wv", wv, w_raw[0])
            for n in range(2):
                wait_filled(act, ("C", n))
                nc.scalar.copy(cw[0][:, 2 * n:2 * n + 2, 0:2 * NSLOT],
                               bank(("C", n))[:].rearrange("p (c n) -> p c n", c=2)).then_inc(c_hi, 1)
            split_x(1)
            v_to_blocks(0)
            split_weight("wo", wo, w_raw[1])
            for i in range(NT + 1):
                t, u, w = i, i - 1, i - 2
                at, xa, ff = t < NT, 0 <= u, 0 <= w
                q = projection_fills(i)

                def fill(n):
                    if q[n] and q[n][0] == "K":
                        k_to_sbuf(*q[n][1:])

                if at:
                    exp_scores(t, 0)
                if ff:
                    gelu_square(w)
                if at:
                    exp_scores(t, 1)
                    probs_to_sbuf(t, 0)
                if xa:
                    exp_energy(u, 0)
                if at:
                    probs_to_sbuf(t, 1)
                if xa:
                    exp_energy(u, 1)
                if t + 1 < NT:
                    v_to_blocks(t + 1)
                if ff:
                    top8_exp(w)
                if at:
                    exp_scores(t, 2)
                    exp_scores(t, 3)
                if xa:
                    energy_to_sbuf(u, 0)
                fill(0)
                if ff:
                    weights_to_sbuf(w)
                if at:
                    probs_to_sbuf(t, 2)
                if xa:
                    energy_to_sbuf(u, 1)
                if at:
                    probs_to_sbuf(t, 3)
                fill(1)
                fill(2)
                if at:
                    o_upper(t)
                if xa:
                    h_upper(u)
                fill(3)
                if i % 2 == 1 and (i + 1) // 2 + 1 < NG:
                    split_x((i + 1) // 2 + 1)
            act.wait_ge(lv_in, 1)
            nc.scalar.activation(lv[:], vh[:, 1, :], ACT.Ln, bias=1.0, accum_out=lsum[:]).then_inc(lv_ready, 1)
            gelu_square(NT - 1)
            top8_exp(NT - 1)
            act.wait_ge(lrn_ready, NT)
            nc.scalar.activation(ga[:, 1], lrn[:], ACT.Tanh, scale=0.5, bias=hgate_c[:, 0:1]).then_inc(g_tanh1, 1)
            weights_to_sbuf(NT - 1)
            act.wait_ge(g_mid, 1)
            nc.scalar.activation(ga[:, 6], ga[:, 5], ACT.Tanh, scale=hgate_c[:, 1:2],
                                 bias=hgate_c[:, 2:3]).then_inc(g_tanh2, 1)

        @block.vector
        def _(dve):
            chain = [0]

            def link(ins):
                chain[0] += 1
                ins.then_inc(dve_chain, 1)
                dve.wait_ge(dve_chain, chain[0])

            def split_weight(name, halves, raw):
                dve.wait_ge(w_hi[name], 1)
                for c in range(KC):
                    last = nc.vector.tensor_tensor(halves[1][:, c, :], raw[:, c, :], halves[0][:, c, :].bitcast(F32),
                                                   ALU.subtract)
                last.then_inc(w_lo[name], 1)

            def q_to_sbuf(g, hg):
                key = ("Q", g, hg)
                wait_filled(dve, key)
                nc.vector.tensor_scalar(qt[:, hg, :], bank(key)[:, 0:GW], bias_qkv[:, 0, hg:hg + 1], None,
                                        ALU.add).then_inc(is_drained(key), 1)

            def shift_scores(t, hg):
                key, u = ("S", t, hg), HG * t + hg
                scores = bank(key)[:].rearrange("p (h k) -> p h k", h=HPG)
                wait_filled(dve, key)
                nc.vector.tensor_reduce(smax[:, u % 2], scores, AX.X, ALU.max).then_inc(smax_ready, 1)
                if u >= 2:
                    wait_filled(dve, ("T", (u - 2) // HG, (u - 2) % HG))
                dve.wait_ge(smax_ready, u + 1)
                nc.vector.tensor_tensor(pr[:, u % 2], scores, smax[:, u % 2].unsqueeze(2).to_broadcast([P, HPG, L]),
                                        ALU.subtract).then_inc(is_drained(key), 1)

            def norm_outputs(t, half):
                dve.wait_ge(pv_done, HG * t + 2 * half + 2)
                if t:
                    wait_filled(dve, ("OT", t - 1))
                link(nc.vector.reciprocal(o_rden[:, half], o_view[half][:, :, 2 * HD:VW]))
                nc.vector.tensor_tensor(on[:, half * D // 2:(half + 1) * D // 2].rearrange("p (n h d) -> p n h d", h=2, d=HD),
                                        o_view[half][:, :, 0:2 * HD].rearrange("p n (h d) -> p n h d", h=2),
                                        o_rden[:, half].unsqueeze(3).to_broadcast([P, NP2 // 2, 2, HD]),
                                        ALU.mult).then_inc(o_ready, 1)

            def o_lower(t):
                key = ("OT", t)
                dve.wait_ge(oh_ready, t + 1)
                nc.vector.tensor_tensor(ot[1][:], bank(key)[:].rearrange("p (c q) -> p c q", c=KC),
                                        ot[0][:].bitcast(F32), ALU.subtract).then_inc(is_drained(key), 1)

            def h_lower(u):
                key = ("HT", u)
                dve.wait_ge(hh_ready, u + 1)
                nc.vector.tensor_tensor(ht[1][:], bank(key)[:].rearrange("p (c q) -> p c q", c=KC),
                                        ht[0][:].bitcast(F32), ALU.subtract).then_inc(is_drained(key), 1)

            def statistics(n, t, rows):
                link(nc.vector.bn_stats(st[:, n, t, :], rows))
                nc.vector.bn_aggr(mv[:, n, t, :], st[:, n, t, :]).then_inc(stat[n], 1)

            def normalize(n, t, dst, rows):
                dve.wait_ge(rstd[n], t + 1)
                return nc.vector.tensor_scalar(dst, rows, mv[:, n, t, 0:1], rs[:, n, t:t + 1],
                                               ALU.subtract, ALU.mult)

            def norm1_start(t):
                key = ("WO", t)
                wait_filled(dve, key)
                dve.wait_ge(xb_ready, t + 1)
                nc.vector.tensor_tensor(xs[:, t % 2], bank(key)[:], xs[:, t % 2], ALU.add).then_inc(is_drained(key), 1)
                wait_drained(dve, key)
                statistics(0, t, xs[:, t % 2])

            def norm1_end(t):
                normalize(0, t, xs[:, t % 2], xs[:, t % 2]).then_inc(x1_ready, 1)

            def norm2_start(u):
                wait_filled(dve, ("R", u))
                statistics(1, u, bank(("R", u))[:])

            def norm2_end(u):
                normalize(1, u, h_all[:, u], bank(("R", u))[:]).then_inc(is_drained(("R", u)), 1)

            def energy_max(u, j):
                key = ("E", u, j)
                wait_filled(dve, key)
                link(nc.vector.tensor_reduce(emax[:, j], bank(key)[:].rearrange("p (k m) -> p k m", k=4), AX.X, ALU.max))
                nc.vector.tensor_scalar(enb[:, j], emax[:, j], -L ** -0.5, None, ALU.mult).then_inc(e_max, 1)

            def energy_norm(u, j):
                wait_drained(dve, ("E", u, j))
                link(nc.vector.reciprocal(erd[:, j], esum[:, j]))
                nc.vector.tensor_tensor(pe2[:, j], pe2[:, j], erd[:, j].unsqueeze(2).to_broadcast([P, 4, M]),
                                        ALU.mult).then_inc(e_norm, 1)

            def memory_scores(w):
                key = ("F", w)
                wait_filled(dve, key)
                if w == 0:
                    dve.wait_ge(ld_ff, 16 * N_FF)
                else:
                    dve.wait_ge(th_ready, w)
                nc.vector.tensor_tensor(fs[:], bank(key)[:, 0:NF], bias_f[:], ALU.add).then_inc(is_drained(key), 1)

            def top8(w):
                router = fs[:, 0:NSLOT]
                wait_drained(dve, ("F", w))
                link(nc.vector.max(m8[:], router))
                link(nc.vector.match_replace(rep[:], m8[:], router, TAKEN))
                link(nc.vector.tensor_tensor(rep[:], rep[:], router, ALU.is_equal))
                if w:
                    dve.wait_ge(w_ready, w)
                link(nc.vector.scalar_tensor_tensor(am[:], rep[:], FAR, fs[:, NSLOT:2 * NSLOT], ALU.mult, ALU.add))
                link(nc.vector.tensor_reduce(amx[:, 0:1], am[:], AX.X, ALU.max))
                nc.vector.tensor_scalar(amx[:, 1:2], amx[:, 0:1], -1.0, None, ALU.mult).then_inc(am_ready, 1)

            def uncertainty_in(w):
                dve.wait_ge(sq_ready, w + 1)
                link(nc.vector.tensor_scalar(sq[:], sq[:], GELU_A, 1.0, ALU.mult, ALU.add))
                nc.vector.tensor_tensor(sq[:], sq[:], fs[:, 2 * NSLOT:NF], ALU.mult).then_inc(th_in, 1)

            def uncertainty_out(w):
                dve.wait_ge(th_ready, w + 1)
                link(nc.vector.scalar_tensor_tensor(th[:], th[:], 1.0, fs[:, 2 * NSLOT:NF], ALU.add, ALU.mult))
                nc.vector.tensor_tensor_reduce(out=th[:], in0=th[:], in1=wu2[:], scale=0.5, scalar=0.0, op0=ALU.mult,
                                               op1=ALU.add, accum_out=lrn[:, w:w + 1]).then_inc(lrn_ready, 1)

            link(nc.vector.memset(v_bd[:], 0.0))
            for h in range(2):
                last = nc.vector.memset(v_bd[h * L:(h + 1) * L, :, :, :, 2 * HD + h:2 * HD + h + 1], 1.0)
            last.then_inc(v_bd_zeroed, 1)
            nc.vector.memset(k_bd[:], 0.0).then_inc(k_bd_zeroed, 1)
            split_weight("wk", wk, w_raw[0])
            split_weight("wq", wq, w_raw[1])
            dve.wait_ge(ld_bias, 48)
            for hg in range(HG):
                q_to_sbuf(0, hg)
            dve.wait_ge(ld_xa, 16 * N_XA)
            dve.wait_ge(c_ident, 1)
            nc.vector.tensor_tensor(bd_skip[:], bd_skip[:], ident[:], ALU.add).then_inc(skip_ready, 1)
            wait_filled(dve, ("G",))
            dve.wait_ge(c_bd, 1)
            for b in range(PB):
                blk = slice(b * L, (b + 1) * L)
                last = nc.vector.tensor_copy(bd_g[blk, blk], bank(("G",))[blk, 0:L])
            last.then_inc(is_drained(("G",)), 1)
            dve.wait_ge(c_kk, 1)
            for n in range(2):
                key = ("kk", n)
                wait_filled(dve, key)
                for b in range(PB):
                    blk = slice(b * L, (b + 1) * L)
                    last = nc.vector.tensor_copy(kk_bd[blk, 4 * n:4 * n + 4, b, :],
                                                 bank(key)[blk, :].rearrange("p (t m) -> p t m", t=4))
                last.then_inc(is_drained(key), 1)
            for n in range(2):
                key = ("vt", n)
                wait_filled(dve, key)
                nc.vector.tensor_copy(vt[:, 4 * n:4 * n + 4, :], bank(key)[:].rearrange("p (t c) -> p t c", t=4)
                                      ).then_inc(is_drained(key), 1)
            wait_filled(dve, ("rk1",))
            nc.vector.tensor_copy(rk1, bank(("rk1",))[0:RDIM, 0:NSLOT]).then_inc(is_drained(("rk1",)), 1)
            dve.wait_ge(ld_ff, 16 * N_FF)
            nc.vector.tensor_scalar(rkk[:, NSLOT:2 * NSLOT], akt_raw, BOT ** -0.5, None, ALU.mult)
            wait_filled(dve, ("rk2",))
            nc.vector.tensor_scalar(rkk[:, 0:NSLOT], bank(("rk2",))[0:BOT, 0:NSLOT], RDIM ** -0.5, None,
                                    ALU.mult).then_inc(is_drained(("rk2",)), 1)
            dve.wait_ge(wu1_hi, 1)
            nc.vector.tensor_tensor(cw[1][:, :, 2 * NSLOT:NF], wu1_raw, cw[0][:, :, 2 * NSLOT:NF].bitcast(F32),
                                    ALU.subtract).then_inc(wu1_lo, 1)
            nc.vector.tensor_scalar(hgate_c[:], gate_c[:], 0.5, None, ALU.mult).then_inc(hgate_ready, 1)
            for n in range(2):
                dve.wait_ge(c_hi, n + 1)
                nc.vector.tensor_tensor(cw[1][:, 2 * n:2 * n + 2, 0:2 * NSLOT],
                                        bank(("C", n))[:].rearrange("p (c n) -> p c n", c=2),
                                        cw[0][:, 2 * n:2 * n + 2, 0:2 * NSLOT].bitcast(F32),
                                        ALU.subtract).then_inc(is_drained(("C", n)), 1)
            wait_filled(dve, ("a1",))
            nc.vector.tensor_copy(a1t, bank(("a1",))[0:VB, 0:P]).then_inc(is_drained(("a1",)), 1)
            wait_filled(dve, ("U",))
            nc.vector.tensor_copy(u_val[:], bank(("U",))[:]).then_inc(is_drained(("U",)), 1)

            for i in range(NT + 1):
                t, u, w = i, i - 1, i - 2
                at, xa, ff = t < NT, 0 <= u, 0 <= w
                q = projection_fills(i)

                def fill(n):
                    if q[n] and q[n][0] == "Q":
                        q_to_sbuf(*q[n][1:])

                if xa:
                    norm1_start(u)
                if at:
                    shift_scores(t, 0)
                if xa:
                    norm1_end(u)
                if ff:
                    memory_scores(w)
                if at:
                    shift_scores(t, 1)
                if t == 0:
                    wait_filled(dve, ("bo",))
                    dve.wait_ge(ld_bo, 16)
                    nc.vector.tensor_tensor(bo_all[:], bank(("bo",))[:], bo_all[:], ALU.add
                                            ).then_inc(is_drained(("bo",)), 1)
                if xa:
                    energy_max(u, 0)
                if ff:
                    uncertainty_in(w)
                if xa:
                    energy_max(u, 1)
                if ff:
                    top8(w)
                if xa:
                    energy_norm(u, 0)
                if at:
                    shift_scores(t, 2)
                if xa:
                    energy_norm(u, 1)
                if at:
                    shift_scores(t, 3)
                    norm_outputs(t, 0)
                if ff:
                    uncertainty_out(w)
                fill(0)
                if xa:
                    norm2_start(u)
                fill(1)
                if xa:
                    norm2_end(u)
                if at:
                    norm_outputs(t, 1)
                fill(2)
                if at:
                    o_lower(t)
                if xa:
                    h_lower(u)
                fill(3)

            var, inv = mv[:, 1, :, 1], rs[:, 1, :]
            link(nc.vector.tensor_tensor(vh[:, 0], var, inv, ALU.mult))
            nc.vector.tensor_tensor(vh[:, 1], vh[:, 0], inv, ALU.mult).then_inc(lv_in, 1)
            memory_scores(NT - 1)
            uncertainty_in(NT - 1)
            top8(NT - 1)
            uncertainty_out(NT - 1)
            wait_filled(dve, ("mean",))
            link(nc.vector.tensor_scalar(rmean[:, 0:1], bank(("mean",))[:, 0:1], 1.0 / NTOK, 1e-6, ALU.mult, ALU.add))
            nc.vector.reciprocal(rmean[:, 1:2], rmean[:, 0:1]).then_inc(is_drained(("mean",)), 1)
            wait_drained(dve, ("mean",))
            link(nc.vector.tensor_scalar(ga[:, 0], lv[:], rmean[:, 1:2], 0.5, ALU.mult, ALU.mult))
            dve.wait_ge(g_tanh1, 1)
            link(nc.vector.scalar_tensor_tensor(ga[:, 2], ga[:, 1], 1.25, ga[:, 0], ALU.mult, ALU.add))
            link(nc.vector.tensor_scalar(ga[:, 3], ga[:, 2], 1.25, 0.0, ALU.add, ALU.max))
            link(nc.vector.tensor_scalar(ga[:, 4], ga[:, 3], 5.0, TAU_LOW, ALU.min, ALU.subtract))
            link(nc.vector.tensor_scalar(ga[:, 4], ga[:, 4], 1.0 / (TAU_HIGH - TAU_LOW), 0.0, ALU.mult, ALU.max))
            nc.vector.tensor_scalar(ga[:, 5], ga[:, 4], 1.0, None, ALU.min).then_inc(g_mid, 1)
            dve.wait_ge(w_ready, NT)
            nc.vector.reciprocal(gs[:], wsum[:])
            dve.wait_ge(g_tanh2, 1)
            link(nc.vector.tensor_scalar(ga[:, 8], ga[:, 6], 0.5, 0.5, ALU.mult, ALU.add))
            link(nc.vector.scalar_tensor_tensor(ga[:, 9], ga[:, 8], EARLY_EXIT, ga[:, 8], ALU.is_ge, ALU.mult))
            link(nc.vector.scalar_tensor_tensor(gs[:], gs[:], 0.5, ga[:, 9], ALU.mult, ALU.mult))
            for j in range(NT + 1):
                if j < NT:
                    key = ("AUX", j)
                    wait_filled(dve, key)
                    nc.vector.scalar_tensor_tensor(h_all[:, j], bank(key)[:], gs[:, j:j + 1], h_all[:, j],
                                                   ALU.mult, ALU.add).then_inc(is_drained(key), 1)
                    wait_drained(dve, key)
                    statistics(2, j, h_all[:, j])
                if j:
                    normalize(2, j - 1, h_all[:, j - 1], h_all[:, j - 1]).then_inc(y_ready, 1)

        @block.tensor
        def _(pe):
            def begin(key):
                number, before = place[key]
                if before:
                    pe.wait_ge(drained[number], before)
                return ps[number]

            def end(key, ins):
                ins.then_inc(filled[place[key][0]], 1)

            def product(out_ap, left, right, last_stop=True):
                for n, (lh, rh) in enumerate(SPLIT):
                    for c in range(KC):
                        ins = nc.tensor.matmul(out_ap, left(lh, c), right(rh, c), start=(n == 0 and c == 0),
                                               stop=(n == len(SPLIT) - 1 and c == KC - 1))
                return ins

            def project(key):
                kind, g, hg = key
                w = wk if kind == "K" else wq
                name = "wk" if kind == "K" else "wq"
                b = begin(key)
                if hg == 0:
                    pe.wait_ge(w_lo[name], 1)
                    pe.wait_ge(x_lo, g + 1)
                end(key, product(b[:, 0:GW], lambda s, c: w[s][:, c, hg * P:(hg + 1) * P],
                                 lambda s, c: xt[g % 2][s][:, c, :]))

            def values(t):
                key, g = ("V", t), t // GT
                b = begin(key)
                if t == 0:
                    pe.wait_ge(w_lo["wv"], 1)
                pe.wait_ge(x_lo, g + 1)
                end(key, product(b[:], lambda s, c: xt[g % 2][s][:, c, (t % GT) * P:(t % GT + 1) * P],
                                 lambda s, c: wv[s][:, c, :]))

            def scores(t, hg):
                key, g = ("S", t, hg), t // GT
                b = begin(key)
                if (t, hg) == (0, 0):
                    pe.wait_ge(c_causal, PB)
                wait_drained(pe, ("Q", g, hg))
                if hg == 0:
                    pe.wait_ge(k_bd_loaded, 16 * HPG * (t + 1))
                nc.tensor.matmul(b[:], ident_b[:], causal[:].rearrange("p h k -> p (h k)"), start=True, stop=False,
                                 skip_group_check=True)
                for n in range(PB):
                    q0 = (t % GT) * P + n * L
                    last = nc.tensor.matmul(b[n * L:(n + 1) * L, :], qt[:, hg, q0:q0 + L],
                                            k_bd[:, hg * PB + n].rearrange("p h k -> p (h k)"), start=False, stop=True,
                                            skip_group_check=True)
                end(key, last)

            def turn(key, source, n, rows=None):
                b = begin(key)
                for k in range(n):
                    last = nc.tensor.transpose(b[:, k * P:(k + 1) * P], source(k), ident[:])
                end(key, last)

            def attend(t, hg):
                wait_drained(pe, ("T", t, hg))
                u = HG * t + hg
                if hg == 0:
                    wait_drained(pe, ("V", t))
                if hg % 2 == 0 and t:
                    pe.wait_ge(o_ready, 2 * (t - 1) + hg // 2 + 1)
                for b in range(PB):
                    for k in range(4):
                        last = nc.tensor.matmul(o_view[hg // 2][b * L:(b + 1) * L, 4 * (hg % 2) + k, :],
                                                pt[:, u % 2, k, b * L:(b + 1) * L], v_bd[:, t % 2, b, 4 * hg + k, :],
                                                start=True, stop=True)
                last.then_inc(pv_done, 1)

            def out_projection(t):
                key = ("WO", t)
                b = begin(key)
                if t == 0:
                    pe.wait_ge(w_lo["wo"], 1)
                wait_drained(pe, ("OT", t))
                end(key, product(b[:], lambda s, c: ot[s][:, c, :], lambda s, c: wo[s][:, c, :]))

            def energies(u, j):
                key = ("E", u, j)
                b = begin(key)
                pe.wait_ge(x1_ready, u + 1)
                for k in range(2):
                    n0 = (2 * j + k) * P
                    last = nc.tensor.matmul(b[:, k * PB * M:(k + 1) * PB * M], xs[:, u % 2, n0:n0 + P],
                                            kk_bd[:, u].rearrange("p b m -> p (b m)"), start=True, stop=True)
                end(key, last)

            def mix(u):
                key = ("R", u)
                b = begin(key)
                for j in range(2):
                    wait_drained(pe, ("X", u, j))
                if u == 0:
                    pe.wait_ge(skip_ready, 1)
                nc.tensor.matmul(b[:], bd_skip[:], xs[:, u % 2, :], start=True, stop=False, skip_group_check=True)
                for n in range(PB):
                    last = nc.tensor.matmul(b[n * L:(n + 1) * L, :], vt[:, u, n * L:(n + 1) * L],
                                            pt2[:, n].rearrange("p k q -> p (k q)"), start=False, stop=True,
                                            skip_group_check=True)
                end(key, last)

            def memory(u):
                key = ("F", u)
                b = begin(key)
                wait_drained(pe, ("HT", u))
                if u == 0:
                    pe.wait_ge(wu1_lo, 1)
                end(key, product(b[:, 0:NF], lambda s, c: ht[s][:, c, :], lambda s, c: cw[s][:, c, :]))

            def weight_products(key):
                b = begin(key)
                kind = key[0]
                if kind == "G":
                    pe.wait_ge(ld_xa, 16 * N_XA)
                    for n in range(PB):
                        last = nc.tensor.matmul(b[n * L:(n + 1) * L, 0:L], xk_raw, xq_raw, start=True, stop=True)
                elif kind == "kk":
                    n = key[1]
                    wait_drained(pe, ("G",))
                    last = nc.tensor.matmul(b[:], bd_g[:], ctx_raw[:, 4 * n:4 * n + 4, :].rearrange("p t m -> p (t m)"),
                                            start=True, stop=True)
                elif kind == "vt":
                    for k in range(4):
                        last = nc.tensor.matmul(b[:, k * P:(k + 1) * P], ctx_raw[:, 4 * key[1] + k, :], bd_v[:],
                                                start=True, stop=True)
                elif kind == "rk1":
                    pe.wait_ge(ld_ff, 16 * N_FF)
                    last = nc.tensor.matmul(b[0:RDIM, 0:NSLOT], wrt_raw, akt_raw, start=True, stop=True)
                elif kind == "rk2":
                    wait_drained(pe, ("rk1",))
                    last = nc.tensor.matmul(b[0:BOT, 0:NSLOT], wr_raw, rk1, start=True, stop=True)
                elif kind == "C":
                    wait_drained(pe, ("rk2",))
                    for k in range(2):
                        c = 2 * key[1] + k
                        last = nc.tensor.matmul(b[:, k * 2 * NSLOT:(k + 1) * 2 * NSLOT], fq[:, c * P:(c + 1) * P], rkk,
                                                start=True, stop=True)
                elif kind == "a1":
                    for c in range(KC):
                        last = nc.tensor.matmul(b[0:VB, 0:P], wvd_raw[:, c, :], av_raw[:, c, :], start=(c == 0),
                                                stop=(c == KC - 1))
                elif kind == "U":
                    wait_drained(pe, ("a1",))
                    last = nc.tensor.matmul(b[:], a1t, wvu_raw, start=True, stop=True)
                elif kind == "bo":
                    pe.wait_ge(ld_w["wo"], 16)
                    for c in range(KC):
                        last = nc.tensor.matmul(b[:], bias_qkv[:, 2, c:c + 1].to_broadcast([P, P]), w_raw[1][:, c, :],
                                                start=(c == 0), stop=(c == KC - 1))
                end(key, last)

            pe.wait_ge(ld_bias, 48)
            for key in units:
                kind = key[0]
                if kind in ("K", "Q"):
                    project(key)
                elif kind == "V":
                    values(key[1])
                elif kind == "S":
                    scores(*key[1:])
                elif kind == "T":
                    n = HG * key[1] + key[2]
                    pe.wait_ge(probs_ready, n + 1)
                    turn(key, lambda k: pr[:, n % 2, 2 * k:2 * k + 2, :].rearrange("p h k -> p (h k)"), 4)
                elif kind == "PV":
                    attend(*key[1:])
                elif kind == "OT":
                    pe.wait_ge(o_ready, 2 * key[1] + 2)
                    turn(key, lambda k: on[:, k * P:(k + 1) * P], KC)
                elif kind == "WO":
                    out_projection(key[1])
                elif kind == "E":
                    energies(*key[1:])
                elif kind == "X":
                    pe.wait_ge(e_norm, 2 * key[1] + key[2] + 1)
                    turn(key, lambda k: pe2[:, key[2], k, :], 4)
                elif kind == "R":
                    mix(key[1])
                elif kind == "HT":
                    wait_drained(pe, ("R", key[1]))
                    turn(key, lambda k: h_all[:, key[1], k * P:(k + 1) * P], KC)
                elif kind == "F":
                    memory(key[1])
                elif kind == "WT":
                    pe.wait_ge(w_ready, key[1] + 1)
                    turn(key, lambda k: wts[:], 1)
                elif kind == "mean":
                    pe.wait_ge(lv_ready, 1)
                    pe.wait_ge(c_ones, 1)
                    end(key, nc.tensor.matmul(begin(key)[:, 0:1], ones[:], lsum[:], start=True, stop=True))
                elif kind == "AUX":
                    b = begin(key)
                    wait_drained(pe, ("WT", key[1]))
                    end(key, nc.tensor.matmul(b[:], wt[:, key[1], :], u_val[:], start=True, stop=True))
                else:
                    weight_products(key)


def kernel(x, ctx_1024, L0_attn_Wq, L0_attn_bq, L0_attn_Wk, L0_attn_bk, L0_attn_Wv, L0_attn_bv, L0_attn_Wo, L0_attn_bo,
           L0_xattn_Wq, L0_xattn_Wk, L0_xattn_Wv, L0_xattn_Wskip, L0_ffn_Wq, L0_ffn_Wr, L0_ffn_aux_keys,
           L0_ffn_aux_values, L0_ffn_Wvd, L0_ffn_Wvu, L0_ffn_Wu1, L0_ffn_bu1, L0_ffn_Wu2, L0_ffn_bu2, L0_ffn_gate_w1,
           L0_ffn_gate_bias, L0_ffn_log_rel):
    import concourse.bacc as bacc
    from concourse.bass_utils import run_bass_kernel_spmd

    def turned(m):
        return np.asarray(m).T

    def columns(v):
        return np.asarray(v).reshape(KC, P).T

    tokens = np.asarray(x).reshape(NTOK, D)
    arrays = {
        "x": tokens, "x_t": tokens.T, "ctx": np.asarray(ctx_1024).reshape(NTOK, M),
        "wq_t": turned(L0_attn_Wq), "wk_t": turned(L0_attn_Wk), "wv_t": turned(L0_attn_Wv), "wo_t": turned(L0_attn_Wo),
        "bq": columns(L0_attn_bq), "bk": columns(L0_attn_bk), "bv": columns(L0_attn_bv),
        "bo": np.asarray(L0_attn_bo).reshape(1, D),
        "xa_wq": L0_xattn_Wq, "xa_wk": L0_xattn_Wk, "xa_wv_t": turned(L0_xattn_Wv), "xa_ws_t": turned(L0_xattn_Wskip),
        "ff_wq": L0_ffn_Wq, "ff_wr": L0_ffn_Wr, "ff_wr_t": turned(L0_ffn_Wr), "ff_ak_t": turned(L0_ffn_aux_keys),
        "ff_av_t": turned(L0_ffn_aux_values), "ff_wvd_t": turned(L0_ffn_Wvd), "ff_wvu_t": turned(L0_ffn_Wvu),
        "ff_wu1_t": turned(L0_ffn_Wu1), "bu1": np.asarray(L0_ffn_bu1).reshape(1, UH),
        "wu2": np.asarray(L0_ffn_Wu2).reshape(1, UH), "bu2": np.asarray(L0_ffn_bu2).reshape(1, 1),
        "gate_w1": np.asarray(L0_ffn_gate_w1).reshape(1, 1), "gate_bias": np.asarray(L0_ffn_gate_bias).reshape(1, 1),
        "log_rel": np.asarray(L0_ffn_log_rel).reshape(1, NSLOT),
    }
    arrays = {name: np.ascontiguousarray(v) for name, v in arrays.items()}
    nc = bacc.Bacc("TRN2", target_bir_lowering=False, num_devices=1)
    aps = {name: nc.dram_tensor("in_" + name, v.shape, F32, kind="ExternalInput").ap() for name, v in arrays.items()}
    out = nc.dram_tensor("out", (NTOK, D), F32, kind="ExternalOutput").ap()
    decoder_block(nc, aps, out)
    r = run_bass_kernel_spmd(nc, [{"in_" + name: v for name, v in arrays.items()}], core_ids=[0])
    return r.results[0]["out"].reshape(B, L, D)
```

```python
from contextlib import ExitStack

import numpy as np
import concourse.bass as bass
from concourse import mybir

F32 = mybir.dt.float32
F32R = mybir.dt.float32r
BF16 = mybir.dt.bfloat16
ALU = mybir.AluOpType
ACT = mybir.ActivationFunctionType
AX = mybir.AxisListType

P = 128
B, L, D = 16, 64, 512
H, HD = 32, 16
M = 128
BOT, RDIM, NSLOT, TOPK, VB, UH = 64, 48, 128, 8, 32, 128
NTOK = B * L
NT = NTOK // P
PB = P // L
KC = D // P
HG = D // P
HPG = P // HD
NP2 = H // 2
GT = 2
GW = GT * P
NG = NT // GT
VW = 2 * HD + 2
NF = 2 * NSLOT + UH
EPS = 1e-5
N_ROW = NF + UH + 3
SMALL = {"xq": (0, L, L), "xk": (L, L, L), "wr": (2 * L, RDIM, BOT), "wrt": (2 * L + BOT, BOT, RDIM),
         "akt": (2 * L + BOT + RDIM, BOT, NSLOT), "wvd": (2 * L + BOT + RDIM + NSLOT, P, KC * VB),
         "end": (2 * L + BOT + RDIM + NSLOT + KC * VB,)}
FAR = -1e30
TAKEN = -3e38
GELU_C = float(np.sqrt(2 / np.pi))
GELU_A = 0.044715
TAU_LOW, TAU_HIGH, EARLY_EXIT = 0.5, 2.0, 0.05
SPLIT = ((0, 0), (0, 1), (1, 0))


def projection_fills(i):
    g = i // 2 + 1
    if i < 0 or g >= NG:
        return [None] * HG
    return [("K" if i % 2 == 0 else "Q", g, hg) for hg in range(HG)]


def tensor_units():
    units = [("K", 0, hg) for hg in range(HG)]
    units += [("Q", 0, hg) for hg in range(HG)] + [("G",), ("rk1",), ("V", 0), ("kk", 0), ("rk2",)]
    q = projection_fills(0)
    units += [("S", 0, 0), ("S", 0, 1), ("V", 1), ("T", 0, 0), ("kk", 1), ("T", 0, 1), ("a1",), ("PV", 0, 0), ("S", 0, 2),
              ("PV", 0, 1), ("S", 0, 3), ("vt", 0), ("U",), q[0], ("T", 0, 2), ("vt", 1), ("T", 0, 3), ("C", 0), q[1],
              ("C", 1), ("PV", 0, 2), ("PV", 0, 3), ("bo",), ("OT", 0), q[2], ("WO", 0), q[3]]
    for i in range(1, NT + 1):
        t, u, w = i, i - 1, i - 2
        at, xa, ff = t < NT, 0 <= u, 0 <= w
        q = projection_fills(i)
        units += [("S", t, 0)] if at else []
        units += [("F", w)] if ff else []
        units += [("S", t, 1)] if at else []
        units += [("E", u, 0)] if xa else []
        units += [("T", t, 0)] if at else []
        units += [("E", u, 1)] if xa else []
        units += [("T", t, 1)] if at else []
        units += [("V", t + 1)] if t + 1 < NT else []
        units += [("PV", t, 0), ("S", t, 2), ("PV", t, 1), ("S", t, 3)] if at else []
        units += [("X", u, 0)] if xa else []
        units += [("WT", w)] if ff else []
        units += [q[0]] if q[0] else []
        units += [("T", t, 2)] if at else []
        units += [("X", u, 1)] if xa else []
        units += [("T", t, 3)] if at else []
        units += [("R", u)] if xa else []
        units += [q[1]] if q[1] else []
        units += [("PV", t, 2), ("PV", t, 3)] if at else []
        units += [q[2]] if q[2] else []
        units += [("OT", t)] if at else []
        units += [("HT", u)] if xa else []
        units += [q[3]] if q[3] else []
        units += [("WO", t)] if at else []
    units += [("F", NT - 1), ("mean",), ("AUX", 0), ("AUX", 1), ("WT", NT - 1)] + [("AUX", j) for j in range(2, NT)]
    return units


BANKS = {"scores": (0, 1), "turned": (2, 3), "products": (4, 5), "opening": range(6)}
OPENING = [("K", 0, hg) for hg in range(HG)] + [("Q", 0, hg) for hg in range(HG)] + [("G",), ("rk1",), ("V", 0), ("kk", 0)]
CLASS_OF = {"S": "scores", "E": "scores", "T": "turned", "X": "turned", "OT": "turned", "HT": "turned",
            "WT": "turned", "rk2": "turned", "a1": "turned"}


def place_units(units):
    place, turn, uses = {}, {c: 0 for c in BANKS}, {}
    for key in units:
        if key[0] == "PV":
            continue
        c = "opening" if key in OPENING else CLASS_OF.get(key[0], "products")
        bank = BANKS[c][turn[c] % len(BANKS[c])]
        turn[c] += 1
        place[key] = (bank, uses.get(bank, 0))
        uses[bank] = uses.get(bank, 0) + 1
    return place


def decoder_block(nc, a, out):
    units = tensor_units()
    place = place_units(units)

    with ExitStack() as ctx:
        def sb(name, shape, dt=F32):
            return ctx.enter_context(nc.sbuf_tensor(name, shape, dt))

        def sem(name):
            return ctx.enter_context(nc.semaphore(name))

        ps = [ctx.enter_context(nc.psum_tensor(f"bank{n}", [P, 512], F32)) for n in range(6)]
        o_ps = [ctx.enter_context(nc.psum_tensor(f"attn_out{n}", [P, 512], F32)) for n in range(2)]
        o_view = [o[:, 0:NP2 // 2 * VW].rearrange("p (n v) -> p n v", v=VW) for o in o_ps]

        ident = sb("ident", [P, P])
        ident_b = sb("ident_b", [P, P], BF16)
        causal = sb("causal", [P, HPG, L], BF16)
        ones = sb("ones", [P, P])
        norm_c = sb("norm_c", [P, 3])
        wk = [sb(f"wk{n}", [P, KC, D], F32R) for n in range(2)]
        wq = [sb(f"wq{n}", [P, KC, D], F32R) for n in range(2)]
        wv = [sb(f"wv{n}", [P, KC, D], F32R) for n in range(2)]
        wo = [sb(f"wo{n}", [P, KC, D], F32R) for n in range(2)]
        bias_qkv = sb("bias_qkv", [P, 3, HG])
        bo_all = sb("bo_all", [P, D])
        kk_bd = sb("kk_bd", [P, NT, PB, M])
        vt = sb("vt", [P, NT, P])
        bd_vs = sb("bd_vs", [P, 2, P])
        bd_g = sb("bd_g", [P, P])
        cw = [sb(f"cw{n}", [P, KC, NF], F32R) for n in range(2)]
        ff_rows = sb("ff_rows", [P, N_ROW])
        bias_f, wu2 = ff_rows[:, 0:NF], ff_rows[:, NF:NF + UH]
        gate_c = ff_rows[:, NF + UH:N_ROW]
        hgate_c = sb("hgate_c", [P, 3])
        u_val = sb("u_val", [P, D])

        xt = [[sb(f"xt{s}{n}", [P, KC, GW], F32R) for n in range(2)] for s in range(2)]
        kt = sb("kt", [P, 2, GT, HG * PB, L])
        qt = sb("qt", [P, HG, GW])
        k_bd = sb("k_bd", [P, HG * PB, HPG, L])
        v_bd = sb("v_bd", [P, 2, PB, NP2, VW])
        smax = sb("smax", [P, 2, HPG])
        pr = sb("pr", [P, 2, HPG, L])
        pt = sb("pt", [P, 2, 4, P])
        o_rden = sb("o_rden", [P, 2, NP2 // 2, 2])
        on = sb("on", [P, D])
        ot = [sb(f"ot{n}", [P, KC, P], F32R) for n in range(2)]
        xs = sb("xs", [P, 2, D])
        st = sb("st", [P, 3, NT, 6])
        mv = sb("mv", [P, 3, NT, 2])
        ve = sb("ve", [P, 3, NT])
        rs = sb("rs", [P, 3, NT])
        emax = sb("emax", [P, 2, 4])
        enb = sb("enb", [P, 2, 4])
        esum = sb("esum", [P, 2, 4])
        erd = sb("erd", [P, 2, 4])
        pe2 = sb("pe2", [P, 2, 4, P])
        pt2 = sb("pt2", [P, PB, KC, P])
        h_all = sb("h_all", [P, NT, D])
        ht = [sb(f"ht{n}", [P, KC, P], F32R) for n in range(2)]
        fs = sb("fs", [P, NF])
        m8 = sb("m8", [P, TOPK])
        rep = sb("rep", [P, NSLOT])
        am = sb("am", [P, NSLOT])
        amx = sb("amx", [P, 2])
        wts = sb("wts", [P, NSLOT])
        sq = sb("sq", [P, UH])
        th = sb("th", [P, UH])
        wt = sb("wt", [P, NT, P])
        wsum = sb("wsum", [P, NT])
        lrn = sb("lrn", [P, NT])
        vh = sb("vh", [P, 2, NT])
        lv = sb("lv", [P, NT])
        lsum = sb("lsum", [P, 1])
        rmean = sb("rmean", [P, 2])
        ga = sb("ga", [P, 10, NT])
        gs = sb("gs", [P, NT])

        w_raw = [h_all[:, 4 * n:4 * n + 4, :] for n in range(2)]
        x_raw = [pt[:].rearrange("p s i q -> p (s i q)").rearrange("p (c n) -> p c n", c=KC)] * 2 + \
                [h_all[:, NT - 2:NT].rearrange("p t n -> p (t n)").rearrange("p (c n) -> p c n", c=KC)] * (NG - 2)
        ctx_raw = pt2[:].rearrange("p b k n -> p (b k) n")
        wu1_raw, av_raw = pe2[:, 0], pe2[:, 1]
        wvu_raw = on[0:VB, :]
        fq = xs[0:BOT, 1, :]
        wt_cols = wt[:].rearrange("p t n -> p (t n)")
        small = wt_cols[:, 0:SMALL["end"][0]]
        xq_raw, xk_raw, wr_raw, wrt_raw, akt_raw, wvd_raw = (small[0:SMALL[n][1], SMALL[n][0]:SMALL[n][0] + SMALL[n][2]]
                                                             for n in ("xq", "xk", "wr", "wrt", "akt", "wvd"))
        wvd_raw = wvd_raw.rearrange("p (c n) -> p c n", c=KC)
        rk1 = wt_cols[0:RDIM, SMALL["end"][0]:SMALL["end"][0] + NSLOT]
        a1t, rkk = th[0:VB, :], fs[0:BOT, 0:2 * NSLOT]

        filled = [sem(f"filled{n}") for n in range(6)]
        drained = [sem(f"drained{n}") for n in range(6)]
        ld_w = {n: [sem(f"ld_{n}_{k}") for k in range(2)] for n in ("wk", "wq", "wv", "wo")}
        ld_x = sem("ld_x")
        ld_xs = [sem(f"ld_xs{n}") for n in range(2)]
        ld_bias = sem("ld_bias")
        ld_bo = sem("ld_bo")
        ld_small = sem("ld_small")
        ld_xa = sem("ld_xa")
        ld_ff = sem("ld_ff")
        ld_rows = sem("ld_rows")
        c_bd = sem("c_bd")
        c_ident = sem("c_ident")
        c_causal = sem("c_causal")
        c_norm = sem("c_norm")
        c_kk = sem("c_kk")
        c_ones = sem("c_ones")
        k_bd_zeroed = sem("k_bd_zeroed")
        v_bd_zeroed = sem("v_bd_zeroed")
        w_hi, w_lo = ({n: sem(f"{n}_{half}") for n in ld_w} for half in ("hi", "lo"))
        x_hi, x_lo = sem("x_hi"), sem("x_lo")
        wu1_hi, wu1_lo = sem("wu1_hi"), sem("wu1_lo")
        c_hi = sem("c_hi")
        skip_ready = sem("skip_ready")
        hgate_ready = sem("hgate_ready")
        k_bd_loaded = sem("k_bd_loaded")
        smax_ready = sem("smax_ready")
        probs_ready = sem("probs_ready")
        pv_done = sem("pv_done")
        o_ready = sem("o_ready")
        oh_ready = sem("oh_ready")
        xb_ready = sem("xb_ready")
        stat = [sem(f"stat{n}") for n in range(3)]
        rstd = [sem(f"rstd{n}") for n in range(3)]
        x1_ready = sem("x1_ready")
        e_max = sem("e_max")
        e_norm = sem("e_norm")
        hh_ready = sem("hh_ready")
        sq_ready = sem("sq_ready")
        th_in, th_ready = sem("th_in"), sem("th_ready")
        am_ready, w_ready = sem("am_ready"), sem("w_ready")
        lrn_ready = sem("lrn_ready")
        lv_in, lv_ready = sem("lv_in"), sem("lv_ready")
        g_tanh1, g_mid, g_tanh2 = sem("g_tanh1"), sem("g_mid"), sem("g_tanh2")
        y_ready = sem("y_ready")
        stored = sem("stored")
        dve_chain, pool_chain = sem("dve_chain"), sem("pool_chain")
        N_XA, N_FF = PB + 1, 4

        def bank(key):
            return ps[place[key][0]]

        def wait_filled(eng, key):
            eng.wait_ge(filled[place[key][0]], place[key][1] + 1)

        def wait_drained(eng, key):
            eng.wait_ge(drained[place[key][0]], place[key][1] + 1)

        def is_drained(key):
            return drained[place[key][0]]

        def load_k_blocks(eng, t):
            g = t // GT
            for hg in range(HG):
                wait_drained(eng, ("K", g, hg))
            if t:
                wait_filled(eng, ("S", t - 1, HG - 1))
            else:
                eng.wait_ge(k_bd_zeroed, 1)
            for j in range(HPG):
                rows = slice(j * HD, (j + 1) * HD)
                eng.dma_start(k_bd[rows, :, j, :], kt[rows, g % 2, t % GT]).then_inc(k_bd_loaded, 16)

        block = ctx.enter_context(nc.Block())

        @block.sync
        def _(sp):
            def load_weight(name, raw):
                for k in range(2):
                    half = slice(k * KC // 2, (k + 1) * KC // 2)
                    sp.dma_start(raw[:, half, :], a[name + "_t"].rearrange("(c p) o -> p c o", p=P)[:, half, :]
                                 ).then_inc(ld_w[name][k], 16)

            def load_xt(g):
                if g:
                    sp.wait_ge(x_lo, g)
                if g == 2:
                    sp.wait_ge(w_lo["wo"], 2)
                    wait_filled(sp, ("bo",))
                sp.dma_start(x_raw[g], a["x_t"].rearrange("(c p) n -> p c n", p=P)[:, :, g * GW:(g + 1) * GW]
                             ).then_inc(ld_x, 16)

            def load_xs(t):
                if t == 1:
                    wait_filled(sp, ("C", 1))
                if t >= 2:
                    wait_filled(sp, ("R", t - 2))
                sp.dma_start(xs[:, t % 2, :], a["x"][t * P:(t + 1) * P, :]).then_inc(ld_xs[t % 2], 16)

            load_xt(0)
            load_weight("wk", w_raw[0])
            load_weight("wq", w_raw[1])
            sp.dma_start(bias_qkv[:].rearrange("p n c -> p (n c)"), a["bias_qkv"]).then_inc(ld_bias, 16)
            sp.dma_start(small, a["small"]).then_inc(ld_small, 16)
            sp.wait_ge(c_bd, 1)
            for b in range(PB):
                blk = slice(b * L, (b + 1) * L)
                sp.dma_start(bd_vs[blk, :, blk], a["xa_vs"].rearrange("r (k n) -> r k n", k=2)).then_inc(ld_xa, 16)
            sp.dma_start(fq, a["ff_wq"]).then_inc(ld_ff, 16)
            sp.dma_start(wvu_raw, a["ff_wvu_t"]).then_inc(ld_ff, 16)
            sp.wait_ge(w_lo["wk"], 2)
            load_weight("wv", w_raw[0])
            sp.wait_ge(w_lo["wq"], 2)
            load_xt(1)
            load_weight("wo", w_raw[1])
            sp.dma_start(ctx_raw, a["ctx"].rearrange("(t p) m -> p t m", p=P)).then_inc(ld_xa, 16)
            load_k_blocks(sp, 0)
            for k, name in enumerate(("ff_wu1_t", "ff_av_t")):
                sp.dma_start(pe2[:, k], a[name].rearrange("(c p) n -> p c n", p=P)).then_inc(ld_ff, 16)
            load_xs(0)
            sp.dma_start(bo_all[:], a["bo"].to_broadcast([P, D])).then_inc(ld_bo, 16)
            sp.dma_start(ff_rows[:], a["ff_rows"].to_broadcast([P, N_ROW])).then_inc(ld_rows, 16)
            for i in range(NT):
                if i + 1 < NT:
                    load_k_blocks(sp, i + 1)
                if i < NT - 1:
                    load_xs(i + 1)
                if i % 2 == 0 and i // 2 + 2 < NG:
                    load_xt(i // 2 + 2)
            for t in range(NT):
                sp.wait_ge(y_ready, t + 1)
                sp.dma_start(out[t * P:(t + 1) * P, :], h_all[:, t, :]).then_inc(stored, 16)
            sp.wait_ge(stored, 16 * NT)

        @block.gpsimd
        def _(pool):
            chain = [0]

            def link(ins):
                chain[0] += 1
                ins.then_inc(pool_chain, 1)
                pool.wait_ge(pool_chain, chain[0])

            nc.gpsimd.memset(bd_g[:], 0.0)
            nc.gpsimd.memset(bd_vs[:], 0.0).then_inc(c_bd, 1)
            link(nc.gpsimd.memset(ident[:], 0.0))
            link(nc.gpsimd.affine_select(out=ident[:], in_=ident[:], compare_op=ALU.not_equal, fill=1.0,
                                         base=0, pattern=[[-1, P]], channel_multiplier=1))
            nc.gpsimd.tensor_copy(ident_b[:], ident[:]).then_inc(c_ident, 1)
            nc.gpsimd.memset(norm_c[:, 0:1], EPS)
            nc.gpsimd.memset(norm_c[:, 1:2], EPS / 4)
            nc.gpsimd.memset(norm_c[:, 2:3], -0.5).then_inc(c_norm, 1)

            def split_x(g):
                pool.wait_ge(x_hi, g + 1)
                nc.gpsimd.tensor_tensor(xt[g % 2][1][:], x_raw[g], xt[g % 2][0][:].bitcast(F32),
                                        ALU.subtract).then_inc(x_lo, 1)

            nc.gpsimd.memset(k_bd[:], 0.0).then_inc(k_bd_zeroed, 1)
            nc.gpsimd.memset(kk_bd[:], 0.0).then_inc(c_kk, 1)
            link(nc.gpsimd.memset(causal[:], 0.0))
            for b in range(PB):
                rows = causal[b * L:(b + 1) * L]
                nc.gpsimd.affine_select(out=rows, in_=rows, compare_op=ALU.is_ge, fill=FAR, base=0,
                                        pattern=[[0, HPG], [-1, L]], channel_multiplier=1).then_inc(c_causal, 1)
                pool.wait_ge(c_causal, b + 1)
            nc.gpsimd.memset(ones[:], 1.0).then_inc(c_ones, 1)
            pool.wait_ge(c_norm, 1)

            def split_weight(name, halves, raw):
                for c in range(KC):
                    pool.wait_ge(w_hi[name], c // 2 + 1)
                    last = nc.gpsimd.tensor_tensor(halves[1][:, c, :], raw[:, c, :], halves[0][:, c, :].bitcast(F32),
                                                   ALU.subtract)
                    if c % 2:
                        last.then_inc(w_lo[name], 1)

            def add_bias(t):
                pool.wait_ge(ld_xs[t % 2], 16 * (t // 2 + 1))
                if t == 0:
                    wait_drained(pool, ("bo",))
                nc.gpsimd.tensor_tensor(xs[:, t % 2, :], xs[:, t % 2, :], bo_all[:], ALU.add).then_inc(xb_ready, 1)

            def inv_std(n, t):
                eps = norm_c[:, 1:2] if n == 2 else norm_c[:, 0:1]
                pool.wait_ge(stat[n], t + 1)
                link(nc.gpsimd.tensor_tensor(ve[:, n, t:t + 1], mv[:, n, t, 1:2], eps, ALU.add))
                nc.gpsimd.tensor_tensor(rs[:, n, t:t + 1], ve[:, n, t:t + 1], norm_c[:, 2:3],
                                        ALU.pow).then_inc(rstd[n], 1)

            split_x(1)
            pool.wait_ge(wu1_hi, 1)
            nc.gpsimd.tensor_tensor(cw[1][:, :, 2 * NSLOT:NF], wu1_raw, cw[0][:, :, 2 * NSLOT:NF].bitcast(F32),
                                    ALU.subtract).then_inc(wu1_lo, 1)
            split_weight("wo", wo, w_raw[1])
            for i in range(NT + 1):
                if i >= 1:
                    inv_std(0, i - 1)
                if i < NT:
                    add_bias(i)
                if i >= 1:
                    inv_std(1, i - 1)
                if i % 2 == 1 and (i + 1) // 2 + 1 < NG:
                    split_x((i + 1) // 2 + 1)
            for t in range(NT):
                inv_std(2, t)

        @block.scalar
        def _(act):
            def split_weight(name, halves, raw):
                for c in range(KC):
                    act.wait_ge(ld_w[name][c // 2], 16)
                    last = nc.scalar.copy(halves[0][:, c, :], raw[:, c, :])
                    if c % 2:
                        last.then_inc(w_hi[name], 1)

            def split_x(g):
                act.wait_ge(ld_x, 16 * (g + 1))
                if g >= 2:
                    wait_filled(act, ("V", GT * (g - 1) - 1))
                nc.scalar.copy(xt[g % 2][0][:], x_raw[g]).then_inc(x_hi, 1)

            def k_to_sbuf(g, hg):
                key = ("K", g, hg)
                wait_filled(act, key)
                if (g, hg) == (0, 0):
                    act.wait_ge(ld_bias, 16)
                if g >= 2 and hg == 0:
                    act.wait_ge(k_bd_loaded, 16 * HPG * GT * (g - 1))
                nc.scalar.activation(kt[:, g % 2, :, hg * PB:(hg + 1) * PB, :].rearrange("p t b k -> p t (b k)"),
                                     bank(key)[:, 0:GW].rearrange("p (t n) -> p t n", t=GT), ACT.Identity,
                                     bias=bias_qkv[:, 1, hg:hg + 1]).then_inc(is_drained(key), 1)

            def v_to_blocks(t):
                key = ("V", t)
                wait_filled(act, key)
                if t == 0:
                    act.wait_ge(v_bd_zeroed, 1)
                if t >= 2:
                    act.wait_ge(pv_done, HG * (t - 1))
                for b in range(PB):
                    for h in range(2):
                        src = bank(key)[b * L:(b + 1) * L, :].rearrange("p (n h d) -> p n h d", h=2, d=HD)[:, :, h, :]
                        dst = v_bd[h * L:(h + 1) * L, t % 2, b, :, h * HD:(h + 1) * HD]
                        last = nc.scalar.copy(dst, src)
                last.then_inc(is_drained(key), 1)

            def exp_scores(t, hg):
                wait_drained(act, ("S", t, hg))
                u = HG * t + hg
                nc.scalar.activation(pr[:, u % 2], pr[:, u % 2], ACT.Exp, scale=HD ** -0.5).then_inc(probs_ready, 1)

            def probs_to_sbuf(t, hg):
                key, u = ("T", t, hg), HG * t + hg
                wait_filled(act, key)
                if u == 0:
                    act.wait_ge(x_lo, 2)
                if u >= 2:
                    act.wait_ge(pv_done, u - 1)
                nc.scalar.copy(pt[:, u % 2], bank(key)[:].rearrange("p (i q) -> p i q", i=4)
                               ).then_inc(is_drained(key), 1)

            def o_upper(t):
                key = ("OT", t)
                wait_filled(act, key)
                if t:
                    wait_filled(act, ("WO", t - 1))
                nc.scalar.copy(ot[0][:], bank(key)[:].rearrange("p (c q) -> p c q", c=KC)).then_inc(oh_ready, 1)

            def h_upper(u):
                key = ("HT", u)
                wait_filled(act, key)
                if u:
                    wait_filled(act, ("F", u - 1))
                nc.scalar.copy(ht[0][:], bank(key)[:].rearrange("p (c q) -> p c q", c=KC)).then_inc(hh_ready, 1)

            def exp_energy(u, j):
                key = ("E", u, j)
                act.wait_ge(e_max, 2 * u + j + 1)
                if u:
                    wait_filled(act, ("X", u - 1, j))
                for k in range(4):
                    last = nc.scalar.activation(pe2[:, j, k, :], bank(key)[:, k * M:(k + 1) * M], ACT.Exp,
                                                bias=enb[:, j, k:k + 1], scale=L ** -0.5,
                                                accum_out=esum[:, j, k:k + 1])
                last.then_inc(is_drained(key), 1)

            def energy_to_sbuf(u, j):
                key = ("X", u, j)
                wait_filled(act, key)
                if u and j == 0:
                    wait_filled(act, ("R", u - 1))
                nc.scalar.copy(pt2[:, :, 2 * j:2 * j + 2, :].rearrange("p b n q -> p n b q"),
                               bank(key)[:].rearrange("p (n b q) -> p n b q", n=2, b=PB)
                               ).then_inc(is_drained(key), 1)

            def gelu_square(w):
                wait_drained(act, ("F", w))
                nc.scalar.activation(sq[:], fs[:, 2 * NSLOT:NF], ACT.Square).then_inc(sq_ready, 1)

            def top8_exp(w):
                act.wait_ge(th_in, w + 1)
                nc.scalar.activation(th[:], sq[:], ACT.Tanh, scale=GELU_C).then_inc(th_ready, 1)
                act.wait_ge(am_ready, w + 1)
                if w:
                    wait_filled(act, ("WT", w - 1))
                nc.scalar.activation(wts[:], am[:], ACT.Exp, bias=amx[:, 1:2], accum_out=wsum[:, w:w + 1]
                                     ).then_inc(w_ready, 1)

            def weights_to_sbuf(w):
                key = ("WT", w)
                wait_filled(act, key)
                nc.scalar.copy(wt[:, w, :], bank(key)[:, 0:P]).then_inc(is_drained(key), 1)

            split_x(0)
            split_weight("wk", wk, w_raw[0])
            split_weight("wq", wq, w_raw[1])
            for hg in range(HG):
                k_to_sbuf(0, hg)
            split_weight("wv", wv, w_raw[0])
            split_x(1)
            split_weight("wo", wo, w_raw[1])
            v_to_blocks(0)
            act.wait_ge(ld_ff, 16 * N_FF)
            nc.scalar.copy(cw[0][:, :, 2 * NSLOT:NF], wu1_raw).then_inc(wu1_hi, 1)

            def c_upper(n):
                wait_filled(act, ("C", n))
                nc.scalar.copy(cw[0][:, 2 * n:2 * n + 2, 0:2 * NSLOT],
                               bank(("C", n))[:].rearrange("p (c n) -> p c n", c=2)).then_inc(c_hi, 1)

            def vt_to_sbuf(n):
                wait_filled(act, ("vt", n))
                nc.scalar.copy(vt[:, 4 * n:4 * n + 4, :], bank(("vt", n))[:].rearrange("p (t c) -> p t c", t=4)
                               ).then_inc(is_drained(("vt", n)), 1)

            for i in range(NT + 1):
                t, u, w = i, i - 1, i - 2
                at, xa, ff = t < NT, 0 <= u, 0 <= w
                q = projection_fills(i)

                def fill(n):
                    if q[n] and q[n][0] == "K":
                        k_to_sbuf(*q[n][1:])

                if at:
                    exp_scores(t, 0)
                if at:
                    exp_scores(t, 1)
                if t == 0:
                    v_to_blocks(1)
                if at:
                    probs_to_sbuf(t, 0)
                if xa:
                    exp_energy(u, 0)
                if ff:
                    gelu_square(w)
                if at:
                    probs_to_sbuf(t, 1)
                if xa:
                    exp_energy(u, 1)
                if 0 < t < NT - 1:
                    v_to_blocks(t + 1)
                if ff:
                    top8_exp(w)
                if at:
                    exp_scores(t, 2)
                if xa:
                    energy_to_sbuf(u, 0)
                if ff:
                    weights_to_sbuf(w)
                if at:
                    exp_scores(t, 3)
                if t == 0:
                    vt_to_sbuf(0)
                    fill(0)
                if at:
                    probs_to_sbuf(t, 2)
                if t != 0:
                    fill(0)
                if xa:
                    energy_to_sbuf(u, 1)
                if t == 0:
                    vt_to_sbuf(1)
                if at:
                    probs_to_sbuf(t, 3)
                if t == 0:
                    c_upper(0)
                fill(1)
                if t == 0:
                    c_upper(1)
                else:
                    fill(2)
                if at:
                    o_upper(t)
                if t == 0:
                    fill(2)
                if xa:
                    h_upper(u)
                fill(3)
                if i % 2 == 1 and (i + 1) // 2 + 1 < NG:
                    split_x((i + 1) // 2 + 1)
            act.wait_ge(lv_in, 1)
            nc.scalar.activation(lv[:], vh[:, 1, :], ACT.Ln, bias=1.0, accum_out=lsum[:]).then_inc(lv_ready, 1)
            gelu_square(NT - 1)
            top8_exp(NT - 1)
            act.wait_ge(lrn_ready, NT)
            nc.scalar.activation(ga[:, 1], lrn[:], ACT.Tanh, scale=0.5, bias=hgate_c[:, 0:1]).then_inc(g_tanh1, 1)
            weights_to_sbuf(NT - 1)
            act.wait_ge(g_mid, 1)
            nc.scalar.activation(ga[:, 6], ga[:, 5], ACT.Tanh, scale=hgate_c[:, 1:2],
                                 bias=hgate_c[:, 2:3]).then_inc(g_tanh2, 1)

        @block.vector
        def _(dve):
            chain = [0]

            def link(ins):
                chain[0] += 1
                ins.then_inc(dve_chain, 1)
                dve.wait_ge(dve_chain, chain[0])

            def split_weight(name, halves, raw):
                for c in range(KC):
                    dve.wait_ge(w_hi[name], c // 2 + 1)
                    last = nc.vector.tensor_tensor(halves[1][:, c, :], raw[:, c, :], halves[0][:, c, :].bitcast(F32),
                                                   ALU.subtract)
                    if c % 2:
                        last.then_inc(w_lo[name], 1)

            def q_to_sbuf(g, hg):
                key = ("Q", g, hg)
                wait_filled(dve, key)
                nc.vector.tensor_scalar(qt[:, hg, :], bank(key)[:, 0:GW], bias_qkv[:, 0, hg:hg + 1], None,
                                        ALU.add).then_inc(is_drained(key), 1)

            def shift_scores(t, hg):
                key, u = ("S", t, hg), HG * t + hg
                scores = bank(key)[:].rearrange("p (h k) -> p h k", h=HPG)
                wait_filled(dve, key)
                nc.vector.tensor_reduce(smax[:, u % 2], scores, AX.X, ALU.max).then_inc(smax_ready, 1)
                if u >= 2:
                    wait_filled(dve, ("T", (u - 2) // HG, (u - 2) % HG))
                dve.wait_ge(smax_ready, u + 1)
                nc.vector.tensor_tensor(pr[:, u % 2], scores, smax[:, u % 2].unsqueeze(2).to_broadcast([P, HPG, L]),
                                        ALU.subtract).then_inc(is_drained(key), 1)

            def norm_outputs(t, half):
                dve.wait_ge(pv_done, HG * t + 2 * half + 2)
                if t:
                    wait_filled(dve, ("OT", t - 1))
                link(nc.vector.reciprocal(o_rden[:, half], o_view[half][:, :, 2 * HD:VW]))
                nc.vector.tensor_tensor(on[:, half * D // 2:(half + 1) * D // 2].rearrange("p (n h d) -> p n h d", h=2, d=HD),
                                        o_view[half][:, :, 0:2 * HD].rearrange("p n (h d) -> p n h d", h=2),
                                        o_rden[:, half].unsqueeze(3).to_broadcast([P, NP2 // 2, 2, HD]),
                                        ALU.mult).then_inc(o_ready, 1)

            def o_lower(t):
                key = ("OT", t)
                dve.wait_ge(oh_ready, t + 1)
                nc.vector.tensor_tensor(ot[1][:], bank(key)[:].rearrange("p (c q) -> p c q", c=KC),
                                        ot[0][:].bitcast(F32), ALU.subtract).then_inc(is_drained(key), 1)

            def h_lower(u):
                key = ("HT", u)
                dve.wait_ge(hh_ready, u + 1)
                nc.vector.tensor_tensor(ht[1][:], bank(key)[:].rearrange("p (c q) -> p c q", c=KC),
                                        ht[0][:].bitcast(F32), ALU.subtract).then_inc(is_drained(key), 1)

            def statistics(n, t, rows):
                link(nc.vector.bn_stats(st[:, n, t, :], rows))
                nc.vector.bn_aggr(mv[:, n, t, :], st[:, n, t, :]).then_inc(stat[n], 1)

            def normalize(n, t, dst, rows):
                dve.wait_ge(rstd[n], t + 1)
                return nc.vector.tensor_scalar(dst, rows, mv[:, n, t, 0:1], rs[:, n, t:t + 1],
                                               ALU.subtract, ALU.mult)

            def norm1_start(t):
                key = ("WO", t)
                wait_filled(dve, key)
                dve.wait_ge(xb_ready, t + 1)
                nc.vector.tensor_tensor(xs[:, t % 2], bank(key)[:], xs[:, t % 2], ALU.add).then_inc(is_drained(key), 1)
                wait_drained(dve, key)
                statistics(0, t, xs[:, t % 2])

            def norm1_end(t):
                normalize(0, t, xs[:, t % 2], xs[:, t % 2]).then_inc(x1_ready, 1)

            def norm2_start(u):
                wait_filled(dve, ("R", u))
                statistics(1, u, bank(("R", u))[:])

            def norm2_end(u):
                normalize(1, u, h_all[:, u], bank(("R", u))[:]).then_inc(is_drained(("R", u)), 1)

            def energy_max(u, j):
                key = ("E", u, j)
                wait_filled(dve, key)
                link(nc.vector.tensor_reduce(emax[:, j], bank(key)[:].rearrange("p (k m) -> p k m", k=4), AX.X, ALU.max))
                nc.vector.tensor_scalar(enb[:, j], emax[:, j], -L ** -0.5, None, ALU.mult).then_inc(e_max, 1)

            def energy_norm(u, j):
                wait_drained(dve, ("E", u, j))
                link(nc.vector.reciprocal(erd[:, j], esum[:, j]))
                nc.vector.tensor_tensor(pe2[:, j], pe2[:, j], erd[:, j].unsqueeze(2).to_broadcast([P, 4, M]),
                                        ALU.mult).then_inc(e_norm, 1)

            def memory_scores(w):
                key = ("F", w)
                wait_filled(dve, key)
                if w == 0:
                    dve.wait_ge(ld_rows, 16)
                    nc.vector.tensor_scalar(hgate_c[:], gate_c, 0.5, None, ALU.mult).then_inc(hgate_ready, 1)
                else:
                    dve.wait_ge(th_ready, w)
                nc.vector.tensor_tensor(fs[:], bank(key)[:, 0:NF], bias_f, ALU.add).then_inc(is_drained(key), 1)

            def top8(w):
                router = fs[:, 0:NSLOT]
                wait_drained(dve, ("F", w))
                link(nc.vector.max(m8[:], router))
                link(nc.vector.match_replace(rep[:], m8[:], router, TAKEN))
                link(nc.vector.tensor_tensor(rep[:], rep[:], router, ALU.is_equal))
                if w:
                    dve.wait_ge(w_ready, w)
                link(nc.vector.scalar_tensor_tensor(am[:], rep[:], FAR, fs[:, NSLOT:2 * NSLOT], ALU.mult, ALU.add))
                link(nc.vector.tensor_reduce(amx[:, 0:1], am[:], AX.X, ALU.max))
                nc.vector.tensor_scalar(amx[:, 1:2], amx[:, 0:1], -1.0, None, ALU.mult).then_inc(am_ready, 1)

            def uncertainty_in(w):
                dve.wait_ge(sq_ready, w + 1)
                link(nc.vector.tensor_scalar(sq[:], sq[:], GELU_A, 1.0, ALU.mult, ALU.add))
                nc.vector.tensor_tensor(sq[:], sq[:], fs[:, 2 * NSLOT:NF], ALU.mult).then_inc(th_in, 1)

            def uncertainty_out(w):
                dve.wait_ge(th_ready, w + 1)
                link(nc.vector.scalar_tensor_tensor(th[:], th[:], 1.0, fs[:, 2 * NSLOT:NF], ALU.add, ALU.mult))
                nc.vector.tensor_tensor_reduce(out=th[:], in0=th[:], in1=wu2, scale=0.5, scalar=0.0, op0=ALU.mult,
                                               op1=ALU.add, accum_out=lrn[:, w:w + 1]).then_inc(lrn_ready, 1)

            link(nc.vector.memset(v_bd[:], 0.0))
            for h in range(2):
                last = nc.vector.memset(v_bd[h * L:(h + 1) * L, :, :, :, 2 * HD + h:2 * HD + h + 1], 1.0)
            last.then_inc(v_bd_zeroed, 1)
            dve.wait_ge(x_hi, 1)
            nc.vector.tensor_tensor(xt[0][1][:], x_raw[0], xt[0][0][:].bitcast(F32), ALU.subtract).then_inc(x_lo, 1)
            split_weight("wk", wk, w_raw[0])
            split_weight("wq", wq, w_raw[1])
            dve.wait_ge(ld_bias, 16)
            for hg in range(HG):
                q_to_sbuf(0, hg)
                if hg == 1:
                    split_weight("wv", wv, w_raw[0])
            wait_filled(dve, ("G",))
            dve.wait_ge(c_bd, 1)
            for b in range(PB):
                blk = slice(b * L, (b + 1) * L)
                last = nc.vector.tensor_copy(bd_g[blk, blk], bank(("G",))[blk, 0:L])
            last.then_inc(is_drained(("G",)), 1)
            wait_filled(dve, ("rk1",))
            nc.vector.tensor_copy(rk1, bank(("rk1",))[0:RDIM, 0:NSLOT]).then_inc(is_drained(("rk1",)), 1)
            dve.wait_ge(ld_xa, 16 * N_XA)
            dve.wait_ge(c_ident, 1)
            nc.vector.tensor_tensor(bd_vs[:, 1], bd_vs[:, 1], ident[:], ALU.add).then_inc(skip_ready, 1)

            def kk_to_blocks(n):
                key = ("kk", n)
                wait_filled(dve, key)
                for b in range(PB):
                    blk = slice(b * L, (b + 1) * L)
                    last = nc.vector.tensor_copy(kk_bd[blk, 4 * n:4 * n + 4, b, :],
                                                 bank(key)[blk, :].rearrange("p (t m) -> p t m", t=4))
                last.then_inc(is_drained(key), 1)


            for i in range(NT + 1):
                t, u, w = i, i - 1, i - 2
                at, xa, ff = t < NT, 0 <= u, 0 <= w
                q = projection_fills(i)

                def fill(n):
                    if q[n] and q[n][0] == "Q":
                        q_to_sbuf(*q[n][1:])

                if xa:
                    norm1_start(u)
                if at:
                    shift_scores(t, 0)
                if xa:
                    norm1_end(u)
                if t == 0:
                    dve.wait_ge(c_kk, 1)
                    kk_to_blocks(0)
                    nc.vector.tensor_scalar(rkk[:, NSLOT:2 * NSLOT], akt_raw, BOT ** -0.5, None, ALU.mult)
                    wait_filled(dve, ("rk2",))
                    nc.vector.tensor_scalar(rkk[:, 0:NSLOT], bank(("rk2",))[0:BOT, 0:NSLOT], RDIM ** -0.5, None,
                                            ALU.mult).then_inc(is_drained(("rk2",)), 1)
                if at:
                    shift_scores(t, 1)
                if t == 0:
                    kk_to_blocks(1)
                    wait_filled(dve, ("a1",))
                    nc.vector.tensor_copy(a1t, bank(("a1",))[0:VB, 0:P]).then_inc(is_drained(("a1",)), 1)
                if xa:
                    energy_max(u, 0)
                if ff:
                    memory_scores(w)
                if xa:
                    energy_max(u, 1)
                if ff:
                    uncertainty_in(w)
                    top8(w)
                if xa:
                    energy_norm(u, 0)
                if at:
                    shift_scores(t, 2)
                if at:
                    shift_scores(t, 3)
                if xa:
                    energy_norm(u, 1)
                if at:
                    if t == 0:
                        wait_filled(dve, ("U",))
                        nc.vector.tensor_copy(u_val[:], bank(("U",))[:]).then_inc(is_drained(("U",)), 1)
                    norm_outputs(t, 0)
                if ff:
                    uncertainty_out(w)
                fill(0)
                if xa:
                    norm2_start(u)
                fill(1)
                if t == 0:
                    for n in range(2):
                        dve.wait_ge(c_hi, n + 1)
                        nc.vector.tensor_tensor(cw[1][:, 2 * n:2 * n + 2, 0:2 * NSLOT],
                                                bank(("C", n))[:].rearrange("p (c n) -> p c n", c=2),
                                                cw[0][:, 2 * n:2 * n + 2, 0:2 * NSLOT].bitcast(F32),
                                                ALU.subtract).then_inc(is_drained(("C", n)), 1)
                if xa:
                    norm2_end(u)
                if at:
                    norm_outputs(t, 1)
                if t == 0:
                    wait_filled(dve, ("bo",))
                    dve.wait_ge(ld_bo, 16)
                    nc.vector.tensor_tensor(bo_all[:], bank(("bo",))[:], bo_all[:], ALU.add
                                            ).then_inc(is_drained(("bo",)), 1)
                fill(2)
                if at:
                    o_lower(t)
                if xa:
                    h_lower(u)
                fill(3)

            var, inv = mv[:, 1, :, 1], rs[:, 1, :]
            link(nc.vector.tensor_tensor(vh[:, 0], var, inv, ALU.mult))
            nc.vector.tensor_tensor(vh[:, 1], vh[:, 0], inv, ALU.mult).then_inc(lv_in, 1)
            memory_scores(NT - 1)
            uncertainty_in(NT - 1)
            top8(NT - 1)
            uncertainty_out(NT - 1)
            wait_filled(dve, ("mean",))
            link(nc.vector.tensor_scalar(rmean[:, 0:1], bank(("mean",))[:, 0:1], 1.0 / NTOK, 1e-6, ALU.mult, ALU.add))
            nc.vector.reciprocal(rmean[:, 1:2], rmean[:, 0:1]).then_inc(is_drained(("mean",)), 1)
            wait_drained(dve, ("mean",))
            link(nc.vector.tensor_scalar(ga[:, 0], lv[:], rmean[:, 1:2], 0.5, ALU.mult, ALU.mult))
            dve.wait_ge(g_tanh1, 1)
            link(nc.vector.scalar_tensor_tensor(ga[:, 2], ga[:, 1], 1.25, ga[:, 0], ALU.mult, ALU.add))
            link(nc.vector.tensor_scalar(ga[:, 3], ga[:, 2], 1.25, 0.0, ALU.add, ALU.max))
            link(nc.vector.tensor_scalar(ga[:, 4], ga[:, 3], 5.0, TAU_LOW, ALU.min, ALU.subtract))
            link(nc.vector.tensor_scalar(ga[:, 4], ga[:, 4], 1.0 / (TAU_HIGH - TAU_LOW), 0.0, ALU.mult, ALU.max))
            nc.vector.tensor_scalar(ga[:, 5], ga[:, 4], 1.0, None, ALU.min).then_inc(g_mid, 1)
            dve.wait_ge(w_ready, NT)
            nc.vector.reciprocal(gs[:], wsum[:])
            dve.wait_ge(g_tanh2, 1)
            link(nc.vector.tensor_scalar(ga[:, 8], ga[:, 6], 0.5, 0.5, ALU.mult, ALU.add))
            link(nc.vector.scalar_tensor_tensor(ga[:, 9], ga[:, 8], EARLY_EXIT, ga[:, 8], ALU.is_ge, ALU.mult))
            link(nc.vector.scalar_tensor_tensor(gs[:], gs[:], 0.5, ga[:, 9], ALU.mult, ALU.mult))
            for j in range(NT + 1):
                if j < NT:
                    key = ("AUX", j)
                    wait_filled(dve, key)
                    nc.vector.scalar_tensor_tensor(h_all[:, j], bank(key)[:], gs[:, j:j + 1], h_all[:, j],
                                                   ALU.mult, ALU.add).then_inc(is_drained(key), 1)
                    wait_drained(dve, key)
                    statistics(2, j, h_all[:, j])
                if j:
                    normalize(2, j - 1, h_all[:, j - 1], h_all[:, j - 1]).then_inc(y_ready, 1)

        @block.tensor
        def _(pe):
            def begin(key):
                number, before = place[key]
                if before:
                    pe.wait_ge(drained[number], before)
                return ps[number]

            def end(key, ins):
                ins.then_inc(filled[place[key][0]], 1)

            def product(out_ap, left, right, operand_waits=None):
                for n, (lh, rh) in enumerate(SPLIT):
                    for c in range(KC):
                        if operand_waits:
                            operand_waits(lh, rh, c)
                        ins = nc.tensor.matmul(out_ap, left(lh, c), right(rh, c), start=(n == 0 and c == 0),
                                               stop=(n == len(SPLIT) - 1 and c == KC - 1))
                return ins

            def project(key):
                kind, g, hg = key
                w = wk if kind == "K" else wq
                name = "wk" if kind == "K" else "wq"
                b = begin(key)

                def operand_waits(w_half, x_half, c):
                    if w_half == x_half == 0 and c == 0:
                        pe.wait_ge(x_hi, g + 1)
                    if x_half == 1 and c == 0:
                        pe.wait_ge(x_lo, g + 1)
                    if g == 0 and c % 2 == 0 and (w_half or not x_half):
                        pe.wait_ge((w_hi, w_lo)[w_half][name], c // 2 + 1)

                end(key, product(b[:, 0:GW], lambda s, c: w[s][:, c, hg * P:(hg + 1) * P],
                                 lambda s, c: xt[g % 2][s][:, c, :], operand_waits if hg == 0 else None))

            def values(t):
                key, g = ("V", t), t // GT
                b = begin(key)
                if t == 0:
                    pe.wait_ge(w_lo["wv"], 2)
                pe.wait_ge(x_lo, g + 1)
                end(key, product(b[:], lambda s, c: xt[g % 2][s][:, c, (t % GT) * P:(t % GT + 1) * P],
                                 lambda s, c: wv[s][:, c, :]))

            def scores(t, hg):
                key, g = ("S", t, hg), t // GT
                b = begin(key)
                if (t, hg) == (0, 0):
                    pe.wait_ge(c_causal, PB)
                wait_drained(pe, ("Q", g, hg))
                if hg == 0:
                    pe.wait_ge(k_bd_loaded, 16 * HPG * (t + 1))
                nc.tensor.matmul(b[:], ident_b[:], causal[:].rearrange("p h k -> p (h k)"), start=True, stop=False,
                                 skip_group_check=True)
                for n in range(PB):
                    q0 = (t % GT) * P + n * L
                    last = nc.tensor.matmul(b[n * L:(n + 1) * L, :], qt[:, hg, q0:q0 + L],
                                            k_bd[:, hg * PB + n].rearrange("p h k -> p (h k)"), start=False, stop=True,
                                            skip_group_check=True)
                end(key, last)

            def turn(key, source, n, rows=None):
                b = begin(key)
                for k in range(n):
                    last = nc.tensor.transpose(b[:, k * P:(k + 1) * P], source(k), ident[:])
                end(key, last)

            def attend(t, hg):
                wait_drained(pe, ("T", t, hg))
                u = HG * t + hg
                if hg == 0:
                    wait_drained(pe, ("V", t))
                if hg % 2 == 0 and t:
                    pe.wait_ge(o_ready, 2 * (t - 1) + hg // 2 + 1)
                for b in range(PB):
                    for k in range(4):
                        last = nc.tensor.matmul(o_view[hg // 2][b * L:(b + 1) * L, 4 * (hg % 2) + k, :],
                                                pt[:, u % 2, k, b * L:(b + 1) * L], v_bd[:, t % 2, b, 4 * hg + k, :],
                                                start=True, stop=True)
                last.then_inc(pv_done, 1)

            def out_projection(t):
                key = ("WO", t)
                b = begin(key)
                if t == 0:
                    pe.wait_ge(w_lo["wo"], 2)
                wait_drained(pe, ("OT", t))
                end(key, product(b[:], lambda s, c: ot[s][:, c, :], lambda s, c: wo[s][:, c, :]))

            def energies(u, j):
                key = ("E", u, j)
                b = begin(key)
                pe.wait_ge(x1_ready, u + 1)
                for k in range(2):
                    n0 = (2 * j + k) * P
                    last = nc.tensor.matmul(b[:, k * PB * M:(k + 1) * PB * M], xs[:, u % 2, n0:n0 + P],
                                            kk_bd[:, u].rearrange("p b m -> p (b m)"), start=True, stop=True)
                end(key, last)

            def mix(u):
                key = ("R", u)
                b = begin(key)
                for j in range(2):
                    wait_drained(pe, ("X", u, j))
                if u == 0:
                    pe.wait_ge(skip_ready, 1)
                nc.tensor.matmul(b[:], bd_vs[:, 1], xs[:, u % 2, :], start=True, stop=False, skip_group_check=True)
                for n in range(PB):
                    last = nc.tensor.matmul(b[n * L:(n + 1) * L, :], vt[:, u, n * L:(n + 1) * L],
                                            pt2[:, n].rearrange("p k q -> p (k q)"), start=False, stop=True,
                                            skip_group_check=True)
                end(key, last)

            def memory(u):
                key = ("F", u)
                b = begin(key)
                wait_drained(pe, ("HT", u))
                if u == 0:
                    pe.wait_ge(wu1_lo, 1)
                end(key, product(b[:, 0:NF], lambda s, c: ht[s][:, c, :], lambda s, c: cw[s][:, c, :]))

            def weight_products(key):
                b = begin(key)
                kind = key[0]
                if kind == "G":
                    pe.wait_ge(ld_small, 16)
                    for n in range(PB):
                        last = nc.tensor.matmul(b[n * L:(n + 1) * L, 0:L], xk_raw, xq_raw, start=True, stop=True)
                elif kind == "kk":
                    n = key[1]
                    wait_drained(pe, ("G",))
                    pe.wait_ge(ld_xa, 16 * N_XA)
                    last = nc.tensor.matmul(b[:], bd_g[:], ctx_raw[:, 4 * n:4 * n + 4, :].rearrange("p t m -> p (t m)"),
                                            start=True, stop=True)
                elif kind == "vt":
                    for k in range(4):
                        last = nc.tensor.matmul(b[:, k * P:(k + 1) * P], ctx_raw[:, 4 * key[1] + k, :], bd_vs[:, 0],
                                                start=True, stop=True)
                elif kind == "rk1":
                    last = nc.tensor.matmul(b[0:RDIM, 0:NSLOT], wrt_raw, akt_raw, start=True, stop=True)
                elif kind == "rk2":
                    wait_drained(pe, ("rk1",))
                    last = nc.tensor.matmul(b[0:BOT, 0:NSLOT], wr_raw, rk1, start=True, stop=True)
                elif kind == "C":
                    wait_drained(pe, ("rk2",))
                    for k in range(2):
                        c = 2 * key[1] + k
                        last = nc.tensor.matmul(b[:, k * 2 * NSLOT:(k + 1) * 2 * NSLOT], fq[:, c * P:(c + 1) * P], rkk,
                                                start=True, stop=True)
                elif kind == "a1":
                    pe.wait_ge(ld_ff, 16 * N_FF)
                    for c in range(KC):
                        last = nc.tensor.matmul(b[0:VB, 0:P], wvd_raw[:, c, :], av_raw[:, c, :], start=(c == 0),
                                                stop=(c == KC - 1))
                elif kind == "U":
                    wait_drained(pe, ("a1",))
                    last = nc.tensor.matmul(b[:], a1t, wvu_raw, start=True, stop=True)
                elif kind == "bo":
                    pe.wait_ge(ld_bias, 16)
                    pe.wait_ge(ld_w["wo"][0], 16)
                    pe.wait_ge(ld_w["wo"][1], 16)
                    for c in range(KC):
                        last = nc.tensor.matmul(b[:], bias_qkv[:, 2, c:c + 1].to_broadcast([P, P]), w_raw[1][:, c, :],
                                                start=(c == 0), stop=(c == KC - 1))
                end(key, last)

            for key in units:
                kind = key[0]
                if kind in ("K", "Q"):
                    project(key)
                elif kind == "V":
                    values(key[1])
                elif kind == "S":
                    scores(*key[1:])
                elif kind == "T":
                    n = HG * key[1] + key[2]
                    pe.wait_ge(probs_ready, n + 1)
                    turn(key, lambda k: pr[:, n % 2, 2 * k:2 * k + 2, :].rearrange("p h k -> p (h k)"), 4)
                elif kind == "PV":
                    attend(*key[1:])
                elif kind == "OT":
                    pe.wait_ge(o_ready, 2 * key[1] + 2)
                    turn(key, lambda k: on[:, k * P:(k + 1) * P], KC)
                elif kind == "WO":
                    out_projection(key[1])
                elif kind == "E":
                    energies(*key[1:])
                elif kind == "X":
                    pe.wait_ge(e_norm, 2 * key[1] + key[2] + 1)
                    turn(key, lambda k: pe2[:, key[2], k, :], 4)
                elif kind == "R":
                    mix(key[1])
                elif kind == "HT":
                    wait_drained(pe, ("R", key[1]))
                    turn(key, lambda k: h_all[:, key[1], k * P:(k + 1) * P], KC)
                elif kind == "F":
                    memory(key[1])
                elif kind == "WT":
                    pe.wait_ge(w_ready, key[1] + 1)
                    turn(key, lambda k: wts[:], 1)
                elif kind == "mean":
                    pe.wait_ge(lv_ready, 1)
                    pe.wait_ge(c_ones, 1)
                    end(key, nc.tensor.matmul(begin(key)[:, 0:1], ones[:], lsum[:], start=True, stop=True))
                elif kind == "AUX":
                    b = begin(key)
                    wait_drained(pe, ("WT", key[1]))
                    end(key, nc.tensor.matmul(b[:], wt[:, key[1], :], u_val[:], start=True, stop=True))
                else:
                    weight_products(key)


def kernel(x, ctx_1024, L0_attn_Wq, L0_attn_bq, L0_attn_Wk, L0_attn_bk, L0_attn_Wv, L0_attn_bv, L0_attn_Wo, L0_attn_bo,
           L0_xattn_Wq, L0_xattn_Wk, L0_xattn_Wv, L0_xattn_Wskip, L0_ffn_Wq, L0_ffn_Wr, L0_ffn_aux_keys,
           L0_ffn_aux_values, L0_ffn_Wvd, L0_ffn_Wvu, L0_ffn_Wu1, L0_ffn_bu1, L0_ffn_Wu2, L0_ffn_bu2, L0_ffn_gate_w1,
           L0_ffn_gate_bias, L0_ffn_log_rel):
    import concourse.bacc as bacc
    from concourse.bass_utils import run_bass_kernel_spmd

    def turned(m):
        return np.asarray(m).T

    def columns(v):
        return np.asarray(v).reshape(KC, P).T

    def row(v):
        return np.asarray(v).reshape(1, -1)

    def packed(parts):
        m = np.zeros((P, SMALL["end"][0]), np.float32)
        for name, v in parts.items():
            first, rows, cols = SMALL[name]
            m[0:rows, first:first + cols] = v
        return m

    tokens = np.asarray(x).reshape(NTOK, D)
    arrays = {
        "x": tokens, "x_t": tokens.T, "ctx": np.asarray(ctx_1024).reshape(NTOK, M),
        "wq_t": turned(L0_attn_Wq), "wk_t": turned(L0_attn_Wk), "wv_t": turned(L0_attn_Wv), "wo_t": turned(L0_attn_Wo),
        "bias_qkv": np.concatenate([columns(v) for v in (L0_attn_bq, L0_attn_bk, L0_attn_bv)], axis=1),
        "bo": row(L0_attn_bo), "xa_vs": np.concatenate([turned(L0_xattn_Wv), turned(L0_xattn_Wskip)], axis=1),
        "small": packed({"xq": L0_xattn_Wq, "xk": L0_xattn_Wk, "wr": L0_ffn_Wr, "wrt": turned(L0_ffn_Wr),
                         "akt": turned(L0_ffn_aux_keys),
                         "wvd": turned(L0_ffn_Wvd).reshape(KC, P, VB).transpose(1, 0, 2).reshape(P, KC * VB)}),
        "ff_wq": L0_ffn_Wq, "ff_av_t": turned(L0_ffn_aux_values), "ff_wvu_t": turned(L0_ffn_Wvu),
        "ff_wu1_t": turned(L0_ffn_Wu1),
        "ff_rows": np.concatenate([row(v) for v in (L0_ffn_log_rel, L0_ffn_log_rel, L0_ffn_bu1, L0_ffn_Wu2, L0_ffn_bu2,
                                                    L0_ffn_gate_w1, L0_ffn_gate_bias)], axis=1),
    }
    arrays = {name: np.ascontiguousarray(v) for name, v in arrays.items()}
    nc = bacc.Bacc("TRN2", target_bir_lowering=False, num_devices=1)
    aps = {name: nc.dram_tensor("in_" + name, v.shape, F32, kind="ExternalInput").ap() for name, v in arrays.items()}
    out = nc.dram_tensor("out", (NTOK, D), F32, kind="ExternalOutput").ap()
    decoder_block(nc, aps, out)
    r = run_bass_kernel_spmd(nc, [{"in_" + name: v for name, v in arrays.items()}], core_ids=[0])
    return r.results[0]["out"].reshape(B, L, D)
```

```python
from contextlib import ExitStack

import numpy as np
import concourse.bass as bass
from concourse import mybir

F32 = mybir.dt.float32
F32R = mybir.dt.float32r
BF16 = mybir.dt.bfloat16
ALU = mybir.AluOpType
ACT = mybir.ActivationFunctionType
AX = mybir.AxisListType

P = 128
B, L, D = 16, 64, 512
H, HD = 32, 16
M = 128
BOT, RDIM, NSLOT, TOPK, VB, UH = 64, 48, 128, 8, 32, 128
NTOK = B * L
NT = NTOK // P
PB = P // L
KC = D // P
HG = D // P
HPG = P // HD
NP2 = H // 2
GT = 2
GW = GT * P
NG = NT // GT
VW = 2 * HD + 2
NF = 2 * NSLOT + UH
EPS = 1e-5
N_ROW = NF + UH + 3
SMALL = {"xq": (0, L, L), "xk": (L, L, L), "wr": (2 * L, RDIM, BOT), "wrt": (2 * L + BOT, BOT, RDIM),
         "akt": (2 * L + BOT + RDIM, BOT, NSLOT), "wvd": (2 * L + BOT + RDIM + NSLOT, P, KC * VB),
         "end": (2 * L + BOT + RDIM + NSLOT + KC * VB,)}
FAR = -1e30
TAKEN = -3e38
GELU_C = float(np.sqrt(2 / np.pi))
GELU_A = 0.044715
TAU_LOW, TAU_HIGH, EARLY_EXIT = 0.5, 2.0, 0.05
PARTS = {"wk": HG, "wq": 2, "wv": 2, "wo": 2}
BUSY, QUIET = range(1, NT - 2), range(NT - 2, NT)
LAST_TWO = range(NT - 2, NT)
LAST_NORM = [(0, 1)] + [(t, t) for t in range(2, NT - 2)] + [(NT - 2, NT - 1)]
SHARED = (1, 2, 3, 4)
TAIL = (slice(0, NT - 1), slice(NT - 1, NT))
SPLIT = ((0, 0), (0, 1), (1, 0))


def projection_fills(i):
    g = i // 2 + 1
    if i < 0 or g >= NG:
        return [None] * HG
    return [("K" if i % 2 == 0 else "Q", g, hg) for hg in range(HG)]


def tensor_units():
    units = [("K", 0, hg) for hg in range(HG)]
    units += [("Q", 0, hg) for hg in range(HG)] + [("G",), ("rk1",), ("V", 0), ("kk", 0), ("rk2",)]
    q = projection_fills(0)
    units += [("S", 0, 0), ("S", 0, 1), ("V", 1), ("T", 0, 0), ("kk", 1), ("T", 0, 1), ("a1",), ("PV", 0, 0), ("S", 0, 2),
              ("PV", 0, 1), ("S", 0, 3), ("vt", 0), ("U",), q[0], ("T", 0, 2), ("vt", 1), ("T", 0, 3), ("C", 0), q[1],
              ("C", 1), ("PV", 0, 2), ("PV", 0, 3), ("bo",), ("OT", 0), ("S", 1, 0), ("S", 1, 1), ("WO", 0), q[2]]
    for t in BUSY:
        u, w = t - 1, t - 2
        late, q = projection_fills(u)[3], projection_fills(t)
        units += [("F", w)] if w >= 0 else []
        units += [late, ("E", u, 0), ("T", t, 0), ("E", u, 1), ("T", t, 1), ("V", t + 1), ("PV", t, 0), ("S", t, 2),
                  ("PV", t, 1), ("S", t, 3), ("X", u, 0), q[0], ("T", t, 2), ("X", u, 1), q[1], ("T", t, 3), ("R", u),
                  ("PV", t, 2), ("PV", t, 3)]
        units += [("WT", w)] if w >= 0 else []
        units += [q[2], ("OT", t), ("S", t + 1, 0), ("HT", u), ("S", t + 1, 1), ("WO", t)]
    for t in QUIET:
        u, w = t - 1, t - 2
        units += [projection_fills(u)[3]] if t == QUIET[0] else [("V", t)]
        units += [("S", t, 2), ("T", t, 0), ("E", u, 0), ("S", t, 3), ("T", t, 1), ("E", u, 1), ("PV", t, 0)]
        units += [("F", w), ("PV", t, 1), ("T", t, 2), ("X", u, 0), ("T", t, 3), ("PV", t, 2), ("X", u, 1), ("PV", t, 3), ("R", u)]
        if t + 1 < NT:
            units += [("S", t + 1, 0), ("OT", t), ("WO", t), ("S", t + 1, 1), ("HT", u), ("WT", w)]
        else:
            units += [("OT", t), ("WO", t), ("HT", u), ("AUX", 0), ("WT", w)]
    u = NT - 1
    units += [("E", u, 0), ("E", u, 1), ("F", u - 1), ("X", u, 0), ("X", u, 1), ("AUX", 1), ("R", u), ("WT", u - 1),
              ("AUX", 2), ("HT", u), ("mean",), ("AUX", 3), ("F", u), ("AUX", 4), ("AUX", 5), ("WT", u), ("AUX", 6),
              ("AUX", 7)]
    return units


BANKS = {"scores": (0, 1), "turned": (2, 3), "products": (4, 5), "opening": range(6),
         "memory": (6, 7, 1, 0)}
OPENING = [("K", 0, hg) for hg in range(HG)] + [("Q", 0, hg) for hg in range(HG)] + [("G",), ("rk1",),
           ("V", 0), ("kk", 0)]
CLASS_OF = {"S": "scores", "E": "scores", "R": "scores", "T": "turned", "X": "turned", "OT": "turned", "HT": "turned",
            "WT": "turned", "AUX": "memory", "rk2": "turned", "a1": "turned"}


def place_units(units):
    place, turn, uses = {}, {c: 0 for c in BANKS}, {}
    for key in units:
        if key[0] == "PV":
            continue
        c = "opening" if key in OPENING else CLASS_OF.get(key[0], "products")
        if key[0] == "E" and key[1] + 1 >= QUIET[0]:
            c = "products"
        if key[0] == "F" and QUIET[0] <= key[1] + 2 <= NT:
            c = "scores"
        bank = BANKS[c][turn[c] % len(BANKS[c])]
        turn[c] += 1
        place[key] = (bank, uses.get(bank, 0))
        uses[bank] = uses.get(bank, 0) + 1
    return place


def decoder_block(nc, a, out):
    units = tensor_units()
    place = place_units(units)

    with ExitStack() as ctx:
        def sb(name, shape, dt=F32):
            return ctx.enter_context(nc.sbuf_tensor(name, shape, dt))

        def sem(name):
            return ctx.enter_context(nc.semaphore(name))

        ps = [ctx.enter_context(nc.psum_tensor(f"bank{n}", [P, 512], F32)) for n in range(6)]
        o_ps = [ctx.enter_context(nc.psum_tensor(f"attn_out{n}", [P, 512], F32)) for n in range(2)]
        ps += o_ps
        o_view = [o[:, 0:NP2 // 2 * VW].rearrange("p (n v) -> p n v", v=VW) for o in o_ps]

        ident = sb("ident", [P, P])
        ident_b = sb("ident_b", [P, P], BF16)
        causal = sb("causal", [P, HPG, L], BF16)
        ones = sb("ones", [P, P])
        norm_c = sb("norm_c", [P, 4])
        wk = [sb(f"wk{n}", [P, KC, D], F32R) for n in range(2)]
        wq = [sb(f"wq{n}", [P, KC, D], F32R) for n in range(2)]
        wv = [sb(f"wv{n}", [P, KC, D], F32R) for n in range(2)]
        wo = [sb(f"wo{n}", [P, KC, D], F32R) for n in range(2)]
        bias_qkv = sb("bias_qkv", [P, 3, HG])
        bo_all = sb("bo_all", [P, D])
        kk_bd = sb("kk_bd", [P, NT, PB, M])
        vt = sb("vt", [P, NT, P])
        bd_vs = sb("bd_vs", [P, 2, P])
        bd_g = sb("bd_g", [P, P])
        cw = [sb(f"cw{n}", [P, KC, NF], F32R) for n in range(2)]
        ff_rows = sb("ff_rows", [P, N_ROW])
        bias_f, wu2 = ff_rows[:, 0:NF], ff_rows[:, NF:NF + UH]
        gate_c = ff_rows[:, NF + UH:N_ROW]
        hgate_c = sb("hgate_c", [P, 3])
        u_val = sb("u_val", [P, D])

        xt = [[sb(f"xt{s}{n}", [P, KC, GW], F32R) for n in range(2)] for s in range(2)]
        kt = sb("kt", [P, 2, GT, HG * PB, L])
        qt = sb("qt", [P, HG, GW])
        k_bd = sb("k_bd", [P, HG * PB, HPG, L])
        v_bd = sb("v_bd", [P, 2, PB, NP2, VW])
        smax = sb("smax", [P, 2, HPG])
        pr = sb("pr", [P, 2, HPG, L])
        pt = sb("pt", [P, 2, 4, P])
        o_rden = sb("o_rden", [P, 2, NP2 // 2, 2])
        on = sb("on", [P, D])
        ot = [sb(f"ot{n}", [P, KC, P], F32R) for n in range(2)]
        xs = sb("xs", [P, 2, D])
        st = sb("st", [P, 3, NT, 6])
        mv = sb("mv", [P, 3, NT, 2])
        ve = sb("ve", [P, 3, NT])
        rs = sb("rs", [P, 3, NT])
        emax = sb("emax", [P, 2, 4])
        enb = sb("enb", [P, 2, 4])
        esum = sb("esum", [P, 2, 4])
        erd = sb("erd", [P, 2, 4])
        pe2 = sb("pe2", [P, 2, 4, P])
        pt2 = sb("pt2", [P, PB, KC, P])
        h_all = sb("h_all", [P, NT, D])
        ht = [sb(f"ht{n}", [P, KC, P], F32R) for n in range(2)]
        fs = sb("fs", [P, NF])
        m8 = sb("m8", [P, TOPK])
        rep = sb("rep", [P, NSLOT])
        am = sb("am", [P, NSLOT])
        amx = sb("amx", [P, 2])
        wts = sb("wts", [P, NSLOT])
        sq = sb("sq", [P, UH])
        th = sb("th", [P, UH])
        wt = sb("wt", [P, NT, P])
        wsum = sb("wsum", [P, NT])
        lrn = sb("lrn", [P, NT])
        vh = sb("vh", [P, 2, NT])
        lv = sb("lv", [P, NT])
        lsum = sb("lsum", [P, 2])
        rmean = sb("rmean", [P, 2])
        ga = sb("ga", [P, 10, NT])
        gs = sb("gs", [P, NT])
        neg, nb = sb("neg", [P, NT]), sb("nb", [P, NT])

        gated = [pe2[:, 0].rearrange("p k n -> p (k n)"), pe2[:, 1].rearrange("p k n -> p (k n)"),
                 pt[:, 0].rearrange("p k n -> p (k n)"),
                 pt[:, 1].rearrange("p k n -> p (k n)")]
        w_raw = [h_all[:, 4 * n:4 * n + 4, :] for n in range(2)]
        x_raw = [pt[:].rearrange("p s i q -> p (s i q)").rearrange("p (c n) -> p c n", c=KC)] * 2 + \
                [h_all[:, NT - 2:NT].rearrange("p t n -> p (t n)").rearrange("p (c n) -> p c n", c=KC)] * (NG - 2)
        ctx_raw = pt2[:].rearrange("p b k n -> p (b k) n")
        wu1_raw, av_raw = pe2[:, 0], pe2[:, 1]
        wvu_raw = on[0:VB, :]
        fq = xs[0:BOT, 1, :]
        wt_cols = wt[:].rearrange("p t n -> p (t n)")
        small = wt_cols[:, 0:SMALL["end"][0]]
        xq_raw, xk_raw, wr_raw, wrt_raw, akt_raw, wvd_raw = (small[0:SMALL[n][1], SMALL[n][0]:SMALL[n][0] + SMALL[n][2]]
                                                             for n in ("xq", "xk", "wr", "wrt", "akt", "wvd"))
        wvd_raw = wvd_raw.rearrange("p (c n) -> p c n", c=KC)
        rk1 = wt_cols[0:RDIM, SMALL["end"][0]:SMALL["end"][0] + NSLOT]
        a1t, rkk = th[0:VB, :], fs[0:BOT, 0:2 * NSLOT]

        filled = [sem(f"filled{n}") for n in range(8)]
        drained = [sem(f"drained{n}") for n in range(8)]
        ld_w = {n: [sem(f"ld_{n}_{k}") for k in range(PARTS[n])] for n in PARTS}
        ld_x = sem("ld_x")
        ld_xs = [sem(f"ld_xs{n}") for n in range(2)]
        ld_bias = sem("ld_bias")
        ld_bo = sem("ld_bo")
        ld_small = sem("ld_small")
        ld_xa = sem("ld_xa")
        ld_ff = sem("ld_ff")
        ld_rows = sem("ld_rows")
        c_bd = sem("c_bd")
        c_ident, c_causal, c_norm, c_ones = sem("c_ident"), sem("c_causal"), sem("c_norm"), sem("c_ones")
        c_kk = sem("c_kk")
        k_bd_zeroed = sem("k_bd_zeroed")
        v_bd_zeroed = sem("v_bd_zeroed")
        w_hi, w_lo = ({n: sem(f"{n}_{half}") for n in ld_w} for half in ("hi", "lo"))
        x_hi, x_lo = sem("x_hi"), sem("x_lo")
        wu1_hi, wu1_lo = sem("wu1_hi"), sem("wu1_lo")
        c_hi = sem("c_hi")
        skip_ready = sem("skip_ready")
        hgate_ready = sem("hgate_ready")
        k_bd_loaded = sem("k_bd_loaded")
        smax_ready = sem("smax_ready")
        probs_ready = sem("probs_ready")
        pv_done = sem("pv_done")
        o_ready = sem("o_ready")
        oh_ready = sem("oh_ready")
        xb_ready = sem("xb_ready")
        stat = [sem(f"stat{n}") for n in range(3)]
        rstd = [sem(f"rstd{n}") for n in range(3)]
        x1_ready = sem("x1_ready")
        e_max = sem("e_max")
        e_norm = sem("e_norm")
        hh_ready = sem("hh_ready")
        sq_ready = sem("sq_ready")
        th_in, th_ready = sem("th_in"), sem("th_ready")
        am_ready, w_ready = sem("am_ready"), sem("w_ready")
        lrn_ready = sem("lrn_ready")
        lv_in, lv_ready = sem("lv_in"), sem("lv_ready")
        g_tanh1, g_mid, g_tanh2 = sem("g_tanh1"), sem("g_mid"), sem("g_tanh2")
        gates_ready, shared_ready = sem("gates_ready"), sem("shared_ready")
        f_sums, last_bias = sem("f_sums"), sem("last_bias")
        y_ready, last_ready = sem("y_ready"), sem("last_ready")
        stored = sem("stored")
        dve_chain, pool_chain = sem("dve_chain"), sem("pool_chain")
        N_XA, N_FF = PB + 1, 4

        def bank(key):
            return ps[place[key][0]]

        def wait_filled(eng, key):
            eng.wait_ge(filled[place[key][0]], place[key][1] + 1)

        def wait_drained(eng, key):
            eng.wait_ge(drained[place[key][0]], place[key][1] + 1)

        def is_drained(key):
            return drained[place[key][0]]

        def load_k_blocks(eng, t):
            g = t // GT
            for hg in range(HG):
                wait_drained(eng, ("K", g, hg))
            if t:
                wait_filled(eng, ("S", t - 1, HG - 1))
            else:
                eng.wait_ge(k_bd_zeroed, 1)
            for j in range(HPG):
                rows = slice(j * HD, (j + 1) * HD)
                eng.dma_start(k_bd[rows, :, j, :], kt[rows, g % 2, t % GT]).then_inc(k_bd_loaded, 16)

        def columns(name, k):
            width = D // PARTS[name]
            return slice(k * width, (k + 1) * width)

        block = ctx.enter_context(nc.Block())

        @block.sync
        def _(sp):
            def load_weight(name, raw):
                for k in range(PARTS[name]):
                    cols = columns(name, k)
                    sp.dma_start(raw[:, :, cols], a[name + "_t"].rearrange("(c p) o -> p c o", p=P)[:, :, cols]
                                 ).then_inc(ld_w[name][k], 16)

            def load_xt(g):
                if g:
                    sp.wait_ge(x_lo, g)
                if g == 2:
                    sp.wait_ge(w_lo["wo"], 2)
                    wait_filled(sp, ("bo",))
                sp.dma_start(x_raw[g], a["x_t"].rearrange("(c p) n -> p c n", p=P)[:, :, g * GW:(g + 1) * GW]
                             ).then_inc(ld_x, 16)

            def load_xs(t):
                if t == 1:
                    wait_filled(sp, ("C", 1))
                if t >= 2:
                    wait_filled(sp, ("R", t - 2))
                sp.dma_start(xs[:, t % 2, :], a["x"][t * P:(t + 1) * P, :]).then_inc(ld_xs[t % 2], 16)

            load_xt(0)
            load_weight("wk", w_raw[0])
            load_weight("wq", w_raw[1])
            sp.dma_start(bias_qkv[:].rearrange("p n c -> p (n c)"), a["bias_qkv"]).then_inc(ld_bias, 16)
            sp.dma_start(small, a["small"]).then_inc(ld_small, 16)
            sp.wait_ge(c_bd, 1)
            for b in range(PB):
                blk = slice(b * L, (b + 1) * L)
                sp.dma_start(bd_vs[blk, :, blk], a["xa_vs"].rearrange("r (k n) -> r k n", k=2)).then_inc(ld_xa, 16)
            sp.dma_start(fq, a["ff_wq"]).then_inc(ld_ff, 16)
            sp.dma_start(wvu_raw, a["ff_wvu_t"]).then_inc(ld_ff, 16)
            sp.wait_ge(w_lo["wk"], PARTS["wk"])
            load_weight("wv", w_raw[0])
            sp.wait_ge(w_lo["wq"], 2)
            load_xt(1)
            load_weight("wo", w_raw[1])
            sp.dma_start(ctx_raw, a["ctx"].rearrange("(t p) m -> p t m", p=P)).then_inc(ld_xa, 16)
            load_k_blocks(sp, 0)
            for k, name in enumerate(("ff_wu1_t", "ff_av_t")):
                sp.dma_start(pe2[:, k], a[name].rearrange("(c p) n -> p c n", p=P)).then_inc(ld_ff, 16)
            load_xs(0)
            sp.dma_start(bo_all[:], a["bo"].to_broadcast([P, D])).then_inc(ld_bo, 16)
            sp.dma_start(ff_rows[:], a["ff_rows"].to_broadcast([P, N_ROW])).then_inc(ld_rows, 16)
            for i in range(NT):
                if i + 1 < NT:
                    load_k_blocks(sp, i + 1)
                if i < NT - 1:
                    load_xs(i + 1)
                if i % 2 == 0 and i // 2 + 2 < NG:
                    load_xt(i // 2 + 2)
            for t in range(NT):
                if t in LAST_TWO:
                    sp.wait_ge(last_ready, t - LAST_TWO[0] + 1)
                else:
                    sp.wait_ge(y_ready, t + 1)
                sp.dma_start(out[t * P:(t + 1) * P, :], h_all[:, t, :]).then_inc(stored, 16)
            sp.wait_ge(stored, 16 * NT)

        @block.gpsimd
        def _(pool):
            chain = [0]

            def link(ins):
                chain[0] += 1
                ins.then_inc(pool_chain, 1)
                pool.wait_ge(pool_chain, chain[0])

            nc.gpsimd.memset(bd_g[:], 0.0)
            nc.gpsimd.memset(bd_vs[:], 0.0).then_inc(c_bd, 1)
            link(nc.gpsimd.memset(ident[:], 0.0))
            link(nc.gpsimd.affine_select(out=ident[:], in_=ident[:], compare_op=ALU.not_equal, fill=1.0,
                                         base=0, pattern=[[-1, P]], channel_multiplier=1))
            nc.gpsimd.tensor_copy(ident_b[:], ident[:]).then_inc(c_ident, 1)
            nc.gpsimd.memset(norm_c[:, 0:1], EPS)
            nc.gpsimd.memset(norm_c[:, 1:2], EPS / 4)
            nc.gpsimd.memset(norm_c[:, 3:4], -1.0)
            nc.gpsimd.memset(norm_c[:, 2:3], -0.5).then_inc(c_norm, 1)

            def split_x(g):
                pool.wait_ge(x_hi, g + 1)
                nc.gpsimd.tensor_tensor(xt[g % 2][1][:], x_raw[g], xt[g % 2][0][:].bitcast(F32),
                                        ALU.subtract).then_inc(x_lo, 1)

            nc.gpsimd.memset(k_bd[:], 0.0).then_inc(k_bd_zeroed, 1)
            nc.gpsimd.memset(kk_bd[:], 0.0).then_inc(c_kk, 1)
            link(nc.gpsimd.memset(causal[:], 0.0))
            for b in range(PB):
                rows = causal[b * L:(b + 1) * L]
                nc.gpsimd.affine_select(out=rows, in_=rows, compare_op=ALU.is_ge, fill=FAR, base=0,
                                        pattern=[[0, HPG], [-1, L]], channel_multiplier=1).then_inc(c_causal, 1)
                pool.wait_ge(c_causal, b + 1)
            nc.gpsimd.memset(ones[:], 1.0).then_inc(c_ones, 1)
            pool.wait_ge(c_norm, 1)

            def split_weight(name, halves, raw):
                for k in range(PARTS[name]):
                    cols = columns(name, k)
                    pool.wait_ge(w_hi[name], k + 1)
                    nc.gpsimd.tensor_tensor(halves[1][:, :, cols], raw[:, :, cols], halves[0][:, :, cols].bitcast(F32),
                                            ALU.subtract).then_inc(w_lo[name], 1)

            def add_bias(t):
                pool.wait_ge(ld_xs[t % 2], 16 * (t // 2 + 1))
                if t == 0:
                    wait_drained(pool, ("bo",))
                nc.gpsimd.tensor_tensor(xs[:, t % 2, :], xs[:, t % 2, :], bo_all[:], ALU.add).then_inc(xb_ready, 1)

            def inv_std(n, t, last):
                tiles = slice(t, last + 1)

                def constant(c):
                    return norm_c[:, c:c + 1].to_broadcast([P, last + 1 - t])

                pool.wait_ge(stat[n], last + 1)
                if n == 2 and t not in LAST_TWO:
                    nc.gpsimd.tensor_tensor(neg[:, tiles], constant(3), mv[:, n, tiles, 0], ALU.mult)
                link(nc.gpsimd.tensor_tensor(ve[:, n, tiles], mv[:, n, tiles, 1], constant(1 if n == 2 else 0), ALU.add))
                nc.gpsimd.tensor_tensor(rs[:, n, tiles], ve[:, n, tiles], constant(2),
                                        ALU.pow).then_inc(rstd[n], last + 1 - t)

            split_x(1)
            pool.wait_ge(wu1_hi, 1)
            nc.gpsimd.tensor_tensor(cw[1][:, :, 2 * NSLOT:NF], wu1_raw, cw[0][:, :, 2 * NSLOT:NF].bitcast(F32),
                                    ALU.subtract).then_inc(wu1_lo, 1)
            split_weight("wo", wo, w_raw[1])
            for i in range(NT + 1):
                if i >= 1:
                    inv_std(0, i - 1, i - 1)
                if i < NT:
                    add_bias(i)
                if i >= 1:
                    inv_std(1, i - 1, i - 1)
                if i % 2 == 1 and (i + 1) // 2 + 1 < NG:
                    split_x((i + 1) // 2 + 1)
            for j in SHARED:
                wait_drained(pool, ("AUX", j))
                nc.gpsimd.tensor_tensor(h_all[:, j], gated[j - SHARED[0]], h_all[:, j],
                                        ALU.add).then_inc(shared_ready, 1)
            for t, last in LAST_NORM:
                inv_std(2, t, last)
                if t not in LAST_TWO:
                    tiles = slice(t, last + 1)
                    pool.wait_ge(rstd[2], last + 1)
                    nc.gpsimd.tensor_tensor(nb[:, tiles], neg[:, tiles], rs[:, 2, tiles], ALU.mult
                                            ).then_inc(last_bias, last + 1 - t)

        @block.scalar
        def _(act):
            def split_weight(name, halves, raw):
                for k in range(PARTS[name]):
                    cols = columns(name, k)
                    act.wait_ge(ld_w[name][k], 16)
                    nc.scalar.copy(halves[0][:, :, cols], raw[:, :, cols]).then_inc(w_hi[name], 1)

            def split_x(g):
                act.wait_ge(ld_x, 16 * (g + 1))
                if g >= 2:
                    wait_filled(act, ("V", GT * (g - 1) - 1))
                nc.scalar.copy(xt[g % 2][0][:], x_raw[g]).then_inc(x_hi, 1)

            def k_to_sbuf(g, hg):
                key = ("K", g, hg)
                wait_filled(act, key)
                if (g, hg) == (0, 0):
                    act.wait_ge(ld_bias, 16)
                if g >= 2 and hg == 0:
                    act.wait_ge(k_bd_loaded, 16 * HPG * GT * (g - 1))
                nc.scalar.activation(kt[:, g % 2, :, hg * PB:(hg + 1) * PB, :].rearrange("p t b k -> p t (b k)"),
                                     bank(key)[:, 0:GW].rearrange("p (t n) -> p t n", t=GT), ACT.Identity,
                                     bias=bias_qkv[:, 1, hg:hg + 1]).then_inc(is_drained(key), 1)

            def v_to_blocks(t):
                key = ("V", t)
                wait_filled(act, key)
                if t == 0:
                    act.wait_ge(v_bd_zeroed, 1)
                if t >= 2:
                    act.wait_ge(pv_done, HG * (t - 1))
                for b in range(PB):
                    for h in range(2):
                        src = bank(key)[b * L:(b + 1) * L, :].rearrange("p (n h d) -> p n h d", h=2, d=HD)[:, :, h, :]
                        dst = v_bd[h * L:(h + 1) * L, t % 2, b, :, h * HD:(h + 1) * HD]
                        last = nc.scalar.copy(dst, src)
                last.then_inc(is_drained(key), 1)

            def exp_scores(t, hg):
                wait_drained(act, ("S", t, hg))
                u = HG * t + hg
                nc.scalar.activation(pr[:, u % 2], pr[:, u % 2], ACT.Exp, scale=HD ** -0.5).then_inc(probs_ready, 1)

            def probs_to_sbuf(t, hg):
                key, u = ("T", t, hg), HG * t + hg
                wait_filled(act, key)
                if u == 0:
                    act.wait_ge(x_lo, 2)
                if u >= 2:
                    act.wait_ge(pv_done, u - 1)
                nc.scalar.copy(pt[:, u % 2], bank(key)[:].rearrange("p (i q) -> p i q", i=4)
                               ).then_inc(is_drained(key), 1)

            def o_upper(t):
                key = ("OT", t)
                wait_filled(act, key)
                if t:
                    wait_filled(act, ("WO", t - 1))
                nc.scalar.copy(ot[0][:], bank(key)[:].rearrange("p (c q) -> p c q", c=KC)).then_inc(oh_ready, 1)

            def h_upper(u):
                key = ("HT", u)
                wait_filled(act, key)
                if u:
                    wait_filled(act, ("F", u - 1))
                nc.scalar.copy(ht[0][:], bank(key)[:].rearrange("p (c q) -> p c q", c=KC)).then_inc(hh_ready, 1)

            def exp_energy(u, j):
                key = ("E", u, j)
                act.wait_ge(e_max, 2 * u + j + 1)
                if u:
                    wait_filled(act, ("X", u - 1, j))
                for k in range(4):
                    last = nc.scalar.activation(pe2[:, j, k, :], bank(key)[:, k * M:(k + 1) * M], ACT.Exp,
                                                bias=enb[:, j, k:k + 1], scale=L ** -0.5,
                                                accum_out=esum[:, j, k:k + 1])
                last.then_inc(is_drained(key), 1)

            def energy_to_sbuf(u, j):
                key = ("X", u, j)
                wait_filled(act, key)
                if u and j == 0:
                    wait_filled(act, ("R", u - 1))
                nc.scalar.copy(pt2[:, :, 2 * j:2 * j + 2, :].rearrange("p b n q -> p n b q"),
                               bank(key)[:].rearrange("p (n b q) -> p n b q", n=2, b=PB)
                               ).then_inc(is_drained(key), 1)

            def gelu_square(w):
                wait_drained(act, ("F", w))
                nc.scalar.activation(sq[:], fs[:, 2 * NSLOT:NF], ACT.Square).then_inc(sq_ready, 1)

            def top8_exp(w):
                act.wait_ge(th_in, w + 1)
                nc.scalar.activation(th[:], sq[:], ACT.Tanh, scale=GELU_C).then_inc(th_ready, 1)
                act.wait_ge(am_ready, w + 1)
                if w:
                    wait_filled(act, ("WT", w - 1))
                nc.scalar.activation(wts[:], am[:], ACT.Exp, bias=amx[:, 1:2], accum_out=wsum[:, w:w + 1]
                                     ).then_inc(w_ready, 1)

            def weights_to_sbuf(w):
                key = ("WT", w)
                wait_filled(act, key)
                nc.scalar.copy(wt[:, w, :], bank(key)[:, 0:P]).then_inc(is_drained(key), 1)

            def log_variance(n):
                act.wait_ge(lv_in, n + 1)
                nc.scalar.activation(lv[:, TAIL[n]], vh[:, 1, TAIL[n]], ACT.Ln, bias=1.0, accum_out=lsum[:, n:n + 1]
                                     ).then_inc(lv_ready, 1)

            split_x(0)
            split_weight("wk", wk, w_raw[0])
            split_weight("wq", wq, w_raw[1])
            for hg in range(HG):
                k_to_sbuf(0, hg)
            split_weight("wv", wv, w_raw[0])
            split_x(1)
            split_weight("wo", wo, w_raw[1])
            v_to_blocks(0)
            act.wait_ge(ld_ff, 16 * N_FF)
            nc.scalar.copy(cw[0][:, :, 2 * NSLOT:NF], wu1_raw).then_inc(wu1_hi, 1)

            def c_upper(n):
                wait_filled(act, ("C", n))
                nc.scalar.copy(cw[0][:, 2 * n:2 * n + 2, 0:2 * NSLOT],
                               bank(("C", n))[:].rearrange("p (c n) -> p c n", c=2)).then_inc(c_hi, 1)

            def vt_to_sbuf(n):
                wait_filled(act, ("vt", n))
                nc.scalar.copy(vt[:, 4 * n:4 * n + 4, :], bank(("vt", n))[:].rearrange("p (t c) -> p t c", t=4)
                               ).then_inc(is_drained(("vt", n)), 1)

            def fill(step, n):
                key = projection_fills(step)[n]
                if key[0] == "K":
                    k_to_sbuf(*key[1:])

            for n in range(2):
                exp_scores(0, n)
            probs_to_sbuf(0, 0)
            v_to_blocks(1)
            probs_to_sbuf(0, 1)
            exp_scores(0, 2)
            vt_to_sbuf(0)
            exp_scores(0, 3)
            fill(0, 0)
            probs_to_sbuf(0, 2)
            vt_to_sbuf(1)
            probs_to_sbuf(0, 3)
            c_upper(0)
            fill(0, 1)
            c_upper(1)
            o_upper(0)
            exp_scores(1, 0)
            for t in BUSY:
                u, w = t - 1, t - 2
                exp_scores(t, 1)
                if t == 1:
                    fill(0, 2)
                fill(t - 1, 3)
                probs_to_sbuf(t, 0)
                exp_energy(u, 0)
                if w >= 0:
                    gelu_square(w)
                probs_to_sbuf(t, 1)
                exp_energy(u, 1)
                v_to_blocks(t + 1)
                exp_scores(t, 2)
                energy_to_sbuf(u, 0)
                exp_scores(t, 3)
                probs_to_sbuf(t, 2)
                fill(t, 0)
                energy_to_sbuf(u, 1)
                fill(t, 1)
                probs_to_sbuf(t, 3)
                if w >= 0:
                    top8_exp(w)
                if w >= 0:
                    weights_to_sbuf(w)
                fill(t, 2)
                o_upper(t)
                h_upper(u)
                exp_scores(t + 1, 0)
                if t % 2 == 1 and (t + 1) // 2 + 1 < NG:
                    split_x((t + 1) // 2 + 1)
            for t in QUIET:
                u, w = t - 1, t - 2
                exp_scores(t, 1)
                if t == QUIET[0]:
                    fill(t - 1, 3)
                else:
                    v_to_blocks(t)
                probs_to_sbuf(t, 0)
                exp_scores(t, 2)
                exp_energy(u, 0)
                probs_to_sbuf(t, 1)
                exp_scores(t, 3)
                exp_energy(u, 1)
                probs_to_sbuf(t, 2)
                energy_to_sbuf(u, 0)
                probs_to_sbuf(t, 3)
                gelu_square(w)
                energy_to_sbuf(u, 1)
                o_upper(t)
                if t + 1 < NT:
                    exp_scores(t + 1, 0)
                top8_exp(w)
                h_upper(u)
                weights_to_sbuf(w)
            for n in range(2):
                exp_energy(NT - 1, n)
            for n in range(2):
                energy_to_sbuf(NT - 1, n)
            gelu_square(NT - 2)
            top8_exp(NT - 2)
            log_variance(0)
            weights_to_sbuf(NT - 2)
            log_variance(1)
            h_upper(NT - 1)

            def gate_tanh1(n):
                act.wait_ge(lrn_ready, TAIL[n].stop)
                act.wait_ge(hgate_ready, 1)
                nc.scalar.activation(ga[:, 1, TAIL[n]], lrn[:, TAIL[n]], ACT.Tanh, scale=0.5, bias=hgate_c[:, 0:1]
                                     ).then_inc(g_tanh1, 1)

            def gate_tanh2(n):
                act.wait_ge(g_mid, n + 1)
                nc.scalar.activation(ga[:, 6, TAIL[n]], ga[:, 5, TAIL[n]], ACT.Tanh, scale=hgate_c[:, 1:2],
                                     bias=hgate_c[:, 2:3]).then_inc(g_tanh2, 1)

            def gated_memory(n):
                key = ("AUX", SHARED[n])
                wait_filled(act, key)
                act.wait_ge(gates_ready, 1)
                if n >= 2:
                    act.wait_ge(pv_done, HG * NT)
                nc.scalar.activation(gated[n], bank(key)[:], ACT.Copy, scale=gs[:, SHARED[n]:SHARED[n] + 1]
                                     ).then_inc(is_drained(key), 1)

            def last_normalize(j):
                act.wait_ge(last_bias, j + 1)
                nc.scalar.activation(h_all[:, j], h_all[:, j], ACT.Identity, scale=rs[:, 2, j:j + 1],
                                     bias=nb[:, j:j + 1]).then_inc(y_ready, 1)

            gate_tanh1(0)
            gate_tanh2(0)
            gated_memory(0)
            gelu_square(NT - 1)
            gated_memory(1)
            top8_exp(NT - 1)
            gated_memory(2)
            gate_tanh1(1)
            weights_to_sbuf(NT - 1)
            gated_memory(3)
            gate_tanh2(1)
            for j in range(LAST_TWO[0]):
                last_normalize(j)

        @block.vector
        def _(dve):
            chain = [0]

            def link(ins):
                chain[0] += 1
                ins.then_inc(dve_chain, 1)
                dve.wait_ge(dve_chain, chain[0])

            def split_weight(name, halves, raw):
                for k in range(PARTS[name]):
                    cols = columns(name, k)
                    dve.wait_ge(w_hi[name], k + 1)
                    nc.vector.tensor_tensor(halves[1][:, :, cols], raw[:, :, cols], halves[0][:, :, cols].bitcast(F32),
                                            ALU.subtract).then_inc(w_lo[name], 1)

            def q_to_sbuf(g, hg):
                key = ("Q", g, hg)
                wait_filled(dve, key)
                nc.vector.tensor_scalar(qt[:, hg, :], bank(key)[:, 0:GW], bias_qkv[:, 0, hg:hg + 1], None,
                                        ALU.add).then_inc(is_drained(key), 1)

            def shift_scores(t, hg):
                key, u = ("S", t, hg), HG * t + hg
                scores = bank(key)[:].rearrange("p (h k) -> p h k", h=HPG)
                wait_filled(dve, key)
                nc.vector.tensor_reduce(smax[:, u % 2], scores, AX.X, ALU.max).then_inc(smax_ready, 1)
                if u >= 2:
                    wait_filled(dve, ("T", (u - 2) // HG, (u - 2) % HG))
                dve.wait_ge(smax_ready, u + 1)
                nc.vector.tensor_tensor(pr[:, u % 2], scores, smax[:, u % 2].unsqueeze(2).to_broadcast([P, HPG, L]),
                                        ALU.subtract).then_inc(is_drained(key), 1)

            def norm_outputs(t, half):
                dve.wait_ge(pv_done, HG * t + 2 * half + 2)
                if t:
                    wait_filled(dve, ("OT", t - 1))
                link(nc.vector.reciprocal(o_rden[:, half], o_view[half][:, :, 2 * HD:VW]))
                nc.vector.tensor_tensor(on[:, half * D // 2:(half + 1) * D // 2].rearrange("p (n h d) -> p n h d", h=2, d=HD),
                                        o_view[half][:, :, 0:2 * HD].rearrange("p n (h d) -> p n h d", h=2),
                                        o_rden[:, half].unsqueeze(3).to_broadcast([P, NP2 // 2, 2, HD]),
                                        ALU.mult).then_inc(o_ready, 1)

            def o_lower(t):
                key = ("OT", t)
                dve.wait_ge(oh_ready, t + 1)
                nc.vector.tensor_tensor(ot[1][:], bank(key)[:].rearrange("p (c q) -> p c q", c=KC),
                                        ot[0][:].bitcast(F32), ALU.subtract).then_inc(is_drained(key), 1)

            def h_lower(u):
                key = ("HT", u)
                dve.wait_ge(hh_ready, u + 1)
                nc.vector.tensor_tensor(ht[1][:], bank(key)[:].rearrange("p (c q) -> p c q", c=KC),
                                        ht[0][:].bitcast(F32), ALU.subtract).then_inc(is_drained(key), 1)

            def statistics(n, t, rows):
                link(nc.vector.bn_stats(st[:, n, t, :], rows))
                nc.vector.bn_aggr(mv[:, n, t, :], st[:, n, t, :]).then_inc(stat[n], 1)

            def normalize(n, t, dst, rows):
                dve.wait_ge(rstd[n], t + 1)
                return nc.vector.tensor_scalar(dst, rows, mv[:, n, t, 0:1], rs[:, n, t:t + 1],
                                               ALU.subtract, ALU.mult)

            def norm1_start(t):
                key = ("WO", t)
                wait_filled(dve, key)
                dve.wait_ge(xb_ready, t + 1)
                nc.vector.tensor_tensor(xs[:, t % 2], bank(key)[:], xs[:, t % 2], ALU.add).then_inc(is_drained(key), 1)
                wait_drained(dve, key)
                statistics(0, t, xs[:, t % 2])

            def norm1_end(t):
                normalize(0, t, xs[:, t % 2], xs[:, t % 2]).then_inc(x1_ready, 1)

            def norm2_start(u):
                wait_filled(dve, ("R", u))
                statistics(1, u, bank(("R", u))[:])

            def norm2_end(u):
                normalize(1, u, h_all[:, u], bank(("R", u))[:]).then_inc(is_drained(("R", u)), 1)

            def energy_max(u, j):
                key = ("E", u, j)
                wait_filled(dve, key)
                link(nc.vector.tensor_reduce(emax[:, j], bank(key)[:].rearrange("p (k m) -> p k m", k=4), AX.X, ALU.max))
                nc.vector.tensor_scalar(enb[:, j], emax[:, j], -L ** -0.5, None, ALU.mult).then_inc(e_max, 1)

            def energy_norm(u, j):
                wait_drained(dve, ("E", u, j))
                link(nc.vector.reciprocal(erd[:, j], esum[:, j]))
                nc.vector.tensor_tensor(pe2[:, j], pe2[:, j], erd[:, j].unsqueeze(2).to_broadcast([P, 4, M]),
                                        ALU.mult).then_inc(e_norm, 1)

            def memory_scores(w):
                key = ("F", w)
                wait_filled(dve, key)
                if w == 0:
                    dve.wait_ge(ld_rows, 16)
                    nc.vector.tensor_scalar(hgate_c[:], gate_c, 0.5, None, ALU.mult).then_inc(hgate_ready, 1)
                else:
                    dve.wait_ge(th_ready, w)
                nc.vector.tensor_tensor(fs[:], bank(key)[:, 0:NF], bias_f, ALU.add).then_inc(is_drained(key), 1)

            def top8(w):
                router = fs[:, 0:NSLOT]
                wait_drained(dve, ("F", w))
                link(nc.vector.max(m8[:], router))
                link(nc.vector.match_replace(rep[:], m8[:], router, TAKEN))
                link(nc.vector.tensor_tensor(rep[:], rep[:], router, ALU.is_equal))
                if w:
                    dve.wait_ge(w_ready, w)
                link(nc.vector.scalar_tensor_tensor(am[:], rep[:], FAR, fs[:, NSLOT:2 * NSLOT], ALU.mult, ALU.add))
                link(nc.vector.tensor_reduce(amx[:, 0:1], am[:], AX.X, ALU.max))
                nc.vector.tensor_scalar(amx[:, 1:2], amx[:, 0:1], -1.0, None, ALU.mult).then_inc(am_ready, 1)

            def uncertainty_in(w):
                dve.wait_ge(sq_ready, w + 1)
                link(nc.vector.tensor_scalar(sq[:], sq[:], GELU_A, 1.0, ALU.mult, ALU.add))
                nc.vector.tensor_tensor(sq[:], sq[:], fs[:, 2 * NSLOT:NF], ALU.mult).then_inc(th_in, 1)

            def uncertainty_out(w):
                dve.wait_ge(th_ready, w + 1)
                link(nc.vector.scalar_tensor_tensor(th[:], th[:], 1.0, fs[:, 2 * NSLOT:NF], ALU.add, ALU.mult))
                nc.vector.tensor_tensor_reduce(out=th[:], in0=th[:], in1=wu2, scale=0.5, scalar=0.0, op0=ALU.mult,
                                               op1=ALU.add, accum_out=lrn[:, w:w + 1]).then_inc(lrn_ready, 1)

            link(nc.vector.memset(v_bd[:], 0.0))
            for h in range(2):
                last = nc.vector.memset(v_bd[h * L:(h + 1) * L, :, :, :, 2 * HD + h:2 * HD + h + 1], 1.0)
            last.then_inc(v_bd_zeroed, 1)
            dve.wait_ge(x_hi, 1)
            nc.vector.tensor_tensor(xt[0][1][:], x_raw[0], xt[0][0][:].bitcast(F32), ALU.subtract).then_inc(x_lo, 1)
            split_weight("wk", wk, w_raw[0])
            split_weight("wq", wq, w_raw[1])
            dve.wait_ge(ld_bias, 16)
            for hg in range(HG):
                q_to_sbuf(0, hg)
                if hg == 1:
                    split_weight("wv", wv, w_raw[0])
            wait_filled(dve, ("G",))
            dve.wait_ge(c_bd, 1)
            for b in range(PB):
                blk = slice(b * L, (b + 1) * L)
                last = nc.vector.tensor_copy(bd_g[blk, blk], bank(("G",))[blk, 0:L])
            last.then_inc(is_drained(("G",)), 1)
            wait_filled(dve, ("rk1",))
            nc.vector.tensor_copy(rk1, bank(("rk1",))[0:RDIM, 0:NSLOT]).then_inc(is_drained(("rk1",)), 1)
            dve.wait_ge(ld_xa, 16 * N_XA)
            dve.wait_ge(c_ident, 1)
            nc.vector.tensor_tensor(bd_vs[:, 1], bd_vs[:, 1], ident[:], ALU.add).then_inc(skip_ready, 1)

            def kk_to_blocks(n):
                key = ("kk", n)
                wait_filled(dve, key)
                for b in range(PB):
                    blk = slice(b * L, (b + 1) * L)
                    last = nc.vector.tensor_copy(kk_bd[blk, 4 * n:4 * n + 4, b, :],
                                                 bank(key)[blk, :].rearrange("p (t m) -> p t m", t=4))
                last.then_inc(is_drained(key), 1)


            def fill(step, n):
                key = projection_fills(step)[n]
                if key[0] == "Q":
                    q_to_sbuf(*key[1:])

            shift_scores(0, 0)
            shift_scores(0, 1)
            dve.wait_ge(c_kk, 1)
            kk_to_blocks(0)
            nc.vector.tensor_scalar(rkk[:, NSLOT:2 * NSLOT], akt_raw, BOT ** -0.5, None, ALU.mult)
            wait_filled(dve, ("rk2",))
            nc.vector.tensor_scalar(rkk[:, 0:NSLOT], bank(("rk2",))[0:BOT, 0:NSLOT], RDIM ** -0.5, None,
                                    ALU.mult).then_inc(is_drained(("rk2",)), 1)
            kk_to_blocks(1)
            wait_filled(dve, ("a1",))
            nc.vector.tensor_copy(a1t, bank(("a1",))[0:VB, 0:P]).then_inc(is_drained(("a1",)), 1)
            shift_scores(0, 2)
            shift_scores(0, 3)
            wait_filled(dve, ("U",))
            nc.vector.tensor_copy(u_val[:], bank(("U",))[:]).then_inc(is_drained(("U",)), 1)
            norm_outputs(0, 0)
            fill(0, 0)
            fill(0, 1)
            for n in range(2):
                dve.wait_ge(c_hi, n + 1)
                nc.vector.tensor_tensor(cw[1][:, 2 * n:2 * n + 2, 0:2 * NSLOT],
                                        bank(("C", n))[:].rearrange("p (c n) -> p c n", c=2),
                                        cw[0][:, 2 * n:2 * n + 2, 0:2 * NSLOT].bitcast(F32),
                                        ALU.subtract).then_inc(is_drained(("C", n)), 1)
            norm_outputs(0, 1)
            wait_filled(dve, ("bo",))
            dve.wait_ge(ld_bo, 16)
            nc.vector.tensor_tensor(bo_all[:], bank(("bo",))[:], bo_all[:], ALU.add).then_inc(is_drained(("bo",)), 1)
            o_lower(0)
            shift_scores(1, 0)
            shift_scores(1, 1)
            for t in BUSY:
                u, w = t - 1, t - 2
                norm1_start(u)
                if w >= 0:
                    memory_scores(w)
                norm1_end(u)
                if t == 1:
                    fill(0, 2)
                fill(t - 1, 3)
                for n in range(2):
                    energy_max(u, n)
                for n in range(2):
                    energy_norm(u, n)
                shift_scores(t, 2)
                shift_scores(t, 3)
                norm_outputs(t, 0)
                fill(t, 0)
                if w >= 0:
                    uncertainty_in(w)
                    top8(w)
                fill(t, 1)
                norm2_start(u)
                if w >= 0:
                    uncertainty_out(w)
                norm_outputs(t, 1)
                norm2_end(u)
                fill(t, 2)
                o_lower(t)
                shift_scores(t + 1, 0)
                h_lower(u)
                shift_scores(t + 1, 1)
            for t in QUIET:
                u, w = t - 1, t - 2
                norm1_start(u)
                if t > QUIET[0]:
                    shift_scores(t, 1)
                    h_lower(w)
                norm1_end(u)
                if t == QUIET[0]:
                    fill(t - 1, 3)
                else:
                    uncertainty_out(w - 1)
                shift_scores(t, 2)
                energy_max(u, 0)
                shift_scores(t, 3)
                energy_max(u, 1)
                energy_norm(u, 0)
                norm_outputs(t, 0)
                memory_scores(w)
                energy_norm(u, 1)
                norm_outputs(t, 1)
                top8(w)
                norm2_start(u)
                o_lower(t)
                norm2_end(u)
                if t + 1 < NT:
                    shift_scores(t + 1, 0)
                uncertainty_in(w)
            u, w = NT - 1, NT - 2
            norm1_start(u)
            h_lower(w)
            norm1_end(u)
            uncertainty_out(w - 1)
            for n in range(2):
                energy_max(u, n)
            for n in range(2):
                energy_norm(u, n)
            memory_scores(w)
            top8(w)
            uncertainty_in(w)

            def hidden_variance(n):
                var, inv = mv[:, 1, TAIL[n], 1], rs[:, 1, TAIL[n]]
                link(nc.vector.tensor_tensor(vh[:, 0, TAIL[n]], var, inv, ALU.mult))
                nc.vector.tensor_tensor(vh[:, 1, TAIL[n]], vh[:, 0, TAIL[n]], inv, ALU.mult).then_inc(lv_in, 1)

            hidden_variance(0)
            norm2_start(u)
            uncertainty_out(w)
            norm2_end(u)
            hidden_variance(1)
            h_lower(u)

            def gate_middle(n):
                g = ga[:, :, TAIL[n]]
                link(nc.vector.tensor_scalar(g[:, 0], lv[:, TAIL[n]], rmean[:, 1:2], 0.5, ALU.mult, ALU.mult))
                dve.wait_ge(g_tanh1, n + 1)
                link(nc.vector.scalar_tensor_tensor(g[:, 2], g[:, 1], 1.25, g[:, 0], ALU.mult, ALU.add))
                link(nc.vector.tensor_scalar(g[:, 3], g[:, 2], 1.25, 0.0, ALU.add, ALU.max))
                link(nc.vector.tensor_scalar(g[:, 4], g[:, 3], 5.0, TAU_LOW, ALU.min, ALU.subtract))
                link(nc.vector.tensor_scalar(g[:, 4], g[:, 4], 1.0 / (TAU_HIGH - TAU_LOW), 0.0, ALU.mult, ALU.max))
                nc.vector.tensor_scalar(g[:, 5], g[:, 4], 1.0, None, ALU.min).then_inc(g_mid, 1)

            def gate_end(n):
                g, part = ga[:, :, TAIL[n]], gs[:, TAIL[n]]
                dve.wait_ge(w_ready, TAIL[n].stop)
                nc.vector.reciprocal(part, wsum[:, TAIL[n]])
                dve.wait_ge(g_tanh2, n + 1)
                link(nc.vector.tensor_scalar(g[:, 8], g[:, 6], 0.5, 0.5, ALU.mult, ALU.add))
                link(nc.vector.scalar_tensor_tensor(g[:, 9], g[:, 8], EARLY_EXIT, g[:, 8], ALU.is_ge, ALU.mult))
                nc.vector.scalar_tensor_tensor(part, part, 0.5, g[:, 9], ALU.mult, ALU.mult).then_inc(gates_ready, 1)
                dve.wait_ge(gates_ready, n + 1)

            def add_memory(j):
                key = ("AUX", j)
                if j not in SHARED:
                    wait_filled(dve, key)
                    nc.vector.scalar_tensor_tensor(h_all[:, j], bank(key)[:], gs[:, j:j + 1], h_all[:, j],
                                                   ALU.mult, ALU.add).then_inc(is_drained(key), 1)
                if j:
                    last_sums(j - 1)
                if j > 1:
                    last_moments(j - 2)

            def last_sums(j):
                if j in SHARED:
                    dve.wait_ge(shared_ready, j - SHARED[0] + 1)
                else:
                    wait_drained(dve, ("AUX", j))
                nc.vector.bn_stats(st[:, 2, j, :], h_all[:, j]).then_inc(f_sums, 1)

            def last_moments(j):
                dve.wait_ge(f_sums, j + 1)
                nc.vector.bn_aggr(mv[:, 2, j, :], st[:, 2, j, :]).then_inc(stat[2], 1)

            wait_filled(dve, ("mean",))
            link(nc.vector.tensor_scalar(rmean[:, 0:1], bank(("mean",))[:, 0:1], 1.0 / NTOK, 1e-6, ALU.mult, ALU.add))
            nc.vector.reciprocal(rmean[:, 1:2], rmean[:, 0:1]).then_inc(is_drained(("mean",)), 1)
            wait_drained(dve, ("mean",))
            gate_middle(0)
            gate_end(0)
            memory_scores(NT - 1)
            add_memory(0)
            uncertainty_in(NT - 1)
            top8(NT - 1)
            add_memory(1)
            uncertainty_out(NT - 1)
            add_memory(2)
            gate_middle(1)
            add_memory(3)
            gate_end(1)
            for j in range(4, NT):
                add_memory(j)
            last_sums(NT - 1)
            last_moments(NT - 2)
            last_moments(NT - 1)
            for j in LAST_TWO:
                normalize(2, j, h_all[:, j], h_all[:, j]).then_inc(last_ready, 1)

        @block.tensor
        def _(pe):
            def begin(key):
                number, before = place[key]
                if before:
                    pe.wait_ge(drained[number], before)
                return ps[number]

            def end(key, ins):
                ins.then_inc(filled[place[key][0]], 1)

            def product(out_ap, left, right, operand_waits=None):
                for n, (lh, rh) in enumerate(SPLIT):
                    for c in range(KC):
                        if operand_waits:
                            operand_waits(lh, rh, c)
                        ins = nc.tensor.matmul(out_ap, left(lh, c), right(rh, c), start=(n == 0 and c == 0),
                                               stop=(n == len(SPLIT) - 1 and c == KC - 1))
                return ins

            def project(key):
                kind, g, hg = key
                w = wk if kind == "K" else wq
                name = "wk" if kind == "K" else "wq"
                b = begin(key)
                part = hg * PARTS[name] // HG

                def operand_waits(w_half, x_half, c):
                    if c == 0 and w_half == 0:
                        pe.wait_ge((x_hi, x_lo)[x_half], g + 1)
                    if c == 0 and x_half == 0:
                        pe.wait_ge((w_hi, w_lo)[w_half][name], part + 1)

                end(key, product(b[:, 0:GW], lambda s, c: w[s][:, c, hg * P:(hg + 1) * P],
                                 lambda s, c: xt[g % 2][s][:, c, :], operand_waits))

            def values(t):
                key, g = ("V", t), t // GT
                b = begin(key)
                if t == 0:
                    pe.wait_ge(w_lo["wv"], 2)
                pe.wait_ge(x_lo, g + 1)
                end(key, product(b[:], lambda s, c: xt[g % 2][s][:, c, (t % GT) * P:(t % GT + 1) * P],
                                 lambda s, c: wv[s][:, c, :]))

            def scores(t, hg):
                key, g = ("S", t, hg), t // GT
                b = begin(key)
                if (t, hg) == (0, 0):
                    pe.wait_ge(c_causal, PB)
                wait_drained(pe, ("Q", g, hg))
                if hg == 0:
                    pe.wait_ge(k_bd_loaded, 16 * HPG * (t + 1))
                nc.tensor.matmul(b[:], ident_b[:], causal[:].rearrange("p h k -> p (h k)"), start=True, stop=False,
                                 skip_group_check=True)
                for n in range(PB):
                    q0 = (t % GT) * P + n * L
                    last = nc.tensor.matmul(b[n * L:(n + 1) * L, :], qt[:, hg, q0:q0 + L],
                                            k_bd[:, hg * PB + n].rearrange("p h k -> p (h k)"), start=False, stop=True,
                                            skip_group_check=True)
                end(key, last)

            def turn(key, source, n):
                b = begin(key)
                for k in range(n):
                    last = nc.tensor.transpose(b[:, k * P:(k + 1) * P], source(k), ident[:])
                end(key, last)

            def attend(t, hg):
                wait_drained(pe, ("T", t, hg))
                u = HG * t + hg
                if hg == 0:
                    wait_drained(pe, ("V", t))
                if hg % 2 == 0 and t:
                    pe.wait_ge(o_ready, 2 * (t - 1) + hg // 2 + 1)
                for b in range(PB):
                    for k in range(4):
                        last = nc.tensor.matmul(o_view[hg // 2][b * L:(b + 1) * L, 4 * (hg % 2) + k, :],
                                                pt[:, u % 2, k, b * L:(b + 1) * L], v_bd[:, t % 2, b, 4 * hg + k, :],
                                                start=True, stop=True)
                last.then_inc(pv_done, 1)

            def out_projection(t):
                key = ("WO", t)
                b = begin(key)
                if t == 0:
                    pe.wait_ge(w_lo["wo"], 2)

                def operand_waits(o_half, w_half, c):
                    if c == 0 and o_half == w_half == 0:
                        pe.wait_ge(oh_ready, t + 1)
                    if c == 0 and o_half == 1:
                        wait_drained(pe, ("OT", t))

                end(key, product(b[:], lambda s, c: ot[s][:, c, :], lambda s, c: wo[s][:, c, :], operand_waits))

            def energies(u, j):
                key = ("E", u, j)
                b = begin(key)
                pe.wait_ge(x1_ready, u + 1)
                for k in range(2):
                    n0 = (2 * j + k) * P
                    last = nc.tensor.matmul(b[:, k * PB * M:(k + 1) * PB * M], xs[:, u % 2, n0:n0 + P],
                                            kk_bd[:, u].rearrange("p b m -> p (b m)"), start=True, stop=True)
                end(key, last)

            def mix(u):
                key = ("R", u)
                b = begin(key)
                for j in range(2):
                    wait_drained(pe, ("X", u, j))
                if u == 0:
                    pe.wait_ge(skip_ready, 1)
                nc.tensor.matmul(b[:], bd_vs[:, 1], xs[:, u % 2, :], start=True, stop=False, skip_group_check=True)
                for n in range(PB):
                    last = nc.tensor.matmul(b[n * L:(n + 1) * L, :], vt[:, u, n * L:(n + 1) * L],
                                            pt2[:, n].rearrange("p k q -> p (k q)"), start=False, stop=True,
                                            skip_group_check=True)
                end(key, last)

            def memory(u):
                key = ("F", u)
                b = begin(key)

                def operand_waits(h_half, w_half, c):
                    if c == 0 and h_half == w_half == 0:
                        pe.wait_ge(hh_ready, u + 1)
                    if c == 0 and h_half == 1:
                        wait_drained(pe, ("HT", u))

                if u == 0:
                    pe.wait_ge(wu1_lo, 1)
                end(key, product(b[:, 0:NF], lambda s, c: ht[s][:, c, :], lambda s, c: cw[s][:, c, :], operand_waits))

            def weight_products(key):
                b = begin(key)
                kind = key[0]
                if kind == "G":
                    pe.wait_ge(ld_small, 16)
                    for n in range(PB):
                        last = nc.tensor.matmul(b[n * L:(n + 1) * L, 0:L], xk_raw, xq_raw, start=True, stop=True)
                elif kind == "kk":
                    n = key[1]
                    wait_drained(pe, ("G",))
                    pe.wait_ge(ld_xa, 16 * N_XA)
                    last = nc.tensor.matmul(b[:], bd_g[:], ctx_raw[:, 4 * n:4 * n + 4, :].rearrange("p t m -> p (t m)"),
                                            start=True, stop=True)
                elif kind == "vt":
                    for k in range(4):
                        last = nc.tensor.matmul(b[:, k * P:(k + 1) * P], ctx_raw[:, 4 * key[1] + k, :], bd_vs[:, 0],
                                                start=True, stop=True)
                elif kind == "rk1":
                    last = nc.tensor.matmul(b[0:RDIM, 0:NSLOT], wrt_raw, akt_raw, start=True, stop=True)
                elif kind == "rk2":
                    wait_drained(pe, ("rk1",))
                    last = nc.tensor.matmul(b[0:BOT, 0:NSLOT], wr_raw, rk1, start=True, stop=True)
                elif kind == "C":
                    wait_drained(pe, ("rk2",))
                    for k in range(2):
                        c = 2 * key[1] + k
                        last = nc.tensor.matmul(b[:, k * 2 * NSLOT:(k + 1) * 2 * NSLOT], fq[:, c * P:(c + 1) * P], rkk,
                                                start=True, stop=True)
                elif kind == "a1":
                    pe.wait_ge(ld_ff, 16 * N_FF)
                    for c in range(KC):
                        last = nc.tensor.matmul(b[0:VB, 0:P], wvd_raw[:, c, :], av_raw[:, c, :], start=(c == 0),
                                                stop=(c == KC - 1))
                elif kind == "U":
                    wait_drained(pe, ("a1",))
                    last = nc.tensor.matmul(b[:], a1t, wvu_raw, start=True, stop=True)
                elif kind == "bo":
                    pe.wait_ge(ld_bias, 16)
                    pe.wait_ge(ld_w["wo"][0], 16)
                    pe.wait_ge(ld_w["wo"][1], 16)
                    for c in range(KC):
                        last = nc.tensor.matmul(b[:], bias_qkv[:, 2, c:c + 1].to_broadcast([P, P]), w_raw[1][:, c, :],
                                                start=(c == 0), stop=(c == KC - 1))
                end(key, last)

            for key in units:
                kind = key[0]
                if kind in ("K", "Q"):
                    project(key)
                elif kind == "V":
                    values(key[1])
                elif kind == "S":
                    scores(*key[1:])
                elif kind == "T":
                    n = HG * key[1] + key[2]
                    pe.wait_ge(probs_ready, n + 1)
                    turn(key, lambda k: pr[:, n % 2, 2 * k:2 * k + 2, :].rearrange("p h k -> p (h k)"), 4)
                elif kind == "PV":
                    attend(*key[1:])
                elif kind == "OT":
                    pe.wait_ge(o_ready, 2 * key[1] + 2)
                    turn(key, lambda k: on[:, k * P:(k + 1) * P], KC)
                elif kind == "WO":
                    out_projection(key[1])
                elif kind == "E":
                    energies(*key[1:])
                elif kind == "X":
                    pe.wait_ge(e_norm, 2 * key[1] + key[2] + 1)
                    turn(key, lambda k: pe2[:, key[2], k, :], 4)
                elif kind == "R":
                    mix(key[1])
                elif kind == "HT":
                    wait_drained(pe, ("R", key[1]))
                    turn(key, lambda k: h_all[:, key[1], k * P:(k + 1) * P], KC)
                elif kind == "F":
                    memory(key[1])
                elif kind == "WT":
                    pe.wait_ge(w_ready, key[1] + 1)
                    turn(key, lambda k: wts[:], 1)
                elif kind == "mean":
                    b = begin(key)
                    pe.wait_ge(lv_ready, 2)
                    pe.wait_ge(c_ones, 1)
                    for n in range(2):
                        last = nc.tensor.matmul(b[:, 0:1], ones[:], lsum[:, n:n + 1], start=(n == 0), stop=(n == 1))
                    end(key, last)
                elif kind == "AUX":
                    b = begin(key)
                    if key[1] < 2:
                        pe.wait_ge(o_ready, 2 * (NT - 1) + key[1] + 1)
                    wait_drained(pe, ("WT", key[1]))
                    end(key, nc.tensor.matmul(b[:], wt[:, key[1], :], u_val[:], start=True, stop=True))
                else:
                    weight_products(key)


def kernel(x, ctx_1024, L0_attn_Wq, L0_attn_bq, L0_attn_Wk, L0_attn_bk, L0_attn_Wv, L0_attn_bv, L0_attn_Wo, L0_attn_bo,
           L0_xattn_Wq, L0_xattn_Wk, L0_xattn_Wv, L0_xattn_Wskip, L0_ffn_Wq, L0_ffn_Wr, L0_ffn_aux_keys,
           L0_ffn_aux_values, L0_ffn_Wvd, L0_ffn_Wvu, L0_ffn_Wu1, L0_ffn_bu1, L0_ffn_Wu2, L0_ffn_bu2, L0_ffn_gate_w1,
           L0_ffn_gate_bias, L0_ffn_log_rel):
    import concourse.bacc as bacc
    from concourse.bass_utils import run_bass_kernel_spmd

    def turned(m):
        return np.asarray(m).T

    def columns(v):
        return np.asarray(v).reshape(KC, P).T

    def row(v):
        return np.asarray(v).reshape(1, -1)

    def packed(parts):
        m = np.zeros((P, SMALL["end"][0]), np.float32)
        for name, v in parts.items():
            first, rows, cols = SMALL[name]
            m[0:rows, first:first + cols] = v
        return m

    tokens = np.asarray(x).reshape(NTOK, D)
    arrays = {
        "x": tokens, "x_t": tokens.T, "ctx": np.asarray(ctx_1024).reshape(NTOK, M),
        "wq_t": turned(L0_attn_Wq), "wk_t": turned(L0_attn_Wk), "wv_t": turned(L0_attn_Wv), "wo_t": turned(L0_attn_Wo),
        "bias_qkv": np.concatenate([columns(v) for v in (L0_attn_bq, L0_attn_bk, L0_attn_bv)], axis=1),
        "bo": row(L0_attn_bo), "xa_vs": np.concatenate([turned(L0_xattn_Wv), turned(L0_xattn_Wskip)], axis=1),
        "small": packed({"xq": L0_xattn_Wq, "xk": L0_xattn_Wk, "wr": L0_ffn_Wr, "wrt": turned(L0_ffn_Wr),
                         "akt": turned(L0_ffn_aux_keys),
                         "wvd": turned(L0_ffn_Wvd).reshape(KC, P, VB).transpose(1, 0, 2).reshape(P, KC * VB)}),
        "ff_wq": L0_ffn_Wq, "ff_av_t": turned(L0_ffn_aux_values), "ff_wvu_t": turned(L0_ffn_Wvu),
        "ff_wu1_t": turned(L0_ffn_Wu1),
        "ff_rows": np.concatenate([row(v) for v in (L0_ffn_log_rel, L0_ffn_log_rel, L0_ffn_bu1, L0_ffn_Wu2, L0_ffn_bu2,
                                                    L0_ffn_gate_w1, L0_ffn_gate_bias)], axis=1),
    }
    arrays = {name: np.ascontiguousarray(v) for name, v in arrays.items()}
    nc = bacc.Bacc("TRN2", target_bir_lowering=False, num_devices=1)
    aps = {name: nc.dram_tensor("in_" + name, v.shape, F32, kind="ExternalInput").ap() for name, v in arrays.items()}
    out = nc.dram_tensor("out", (NTOK, D), F32, kind="ExternalOutput").ap()
    decoder_block(nc, aps, out)
    r = run_bass_kernel_spmd(nc, [{"in_" + name: v for name, v in arrays.items()}], core_ids=[0])
    return r.results[0]["out"].reshape(B, L, D)
```
